# Optimizing a Trainium2 kernel written in Bass

```python
import numpy as np
import jax
import jax.numpy as jnp

def _softmax(x, axis=-1):
    return jax.nn.softmax(x, axis=axis)

def _gelu(x):
    return jax.nn.gelu(x, approximate=True)

def _silu(x):
    return jax.nn.silu(x)

def _sigmoid(x):
    return jax.nn.sigmoid(x)

def _layernorm(x, axis=-1, eps=1e-05):
    m = jnp.mean(x, axis=axis, keepdims=True)
    v = jnp.var(x, axis=axis, keepdims=True)
    return (x - m) / jnp.sqrt(v + eps)

def _scatter_add(tgt, idx, src, axis=0):
    return tgt.at[idx].add(src)

def _segment_sum(src, seg, n):
    return jax.ops.segment_sum(src, seg, n)
kernel_name = 'mk_decoder_preln_d1_seqx_r8_ef5d93'

def setup_inputs(seed: int=0):
    np.random.seed(seed)
    _w = jnp.asarray

    def _rec_inputs():
        import jax
        import jax.numpy as jnp
        _rk = jax.random.key(seed)
        x = -0.0002928 + 1 * jax.random.normal(jax.random.fold_in(_rk, 1), (4, 512, 128), jnp.float32)
        _lenS = 512 - jax.random.randint(jax.random.fold_in(_rk, 7), (4,), 0, max(1, 512 // 4) + 1, jnp.int32)
        _lenS2 = 77 - jax.random.randint(jax.random.fold_in(_rk, 8), (4,), 0, max(1, 77 // 4) + 1, jnp.int32)
        _ctx_1024P = jax.random.normal(jax.random.fold_in(_rk, 11), (4, 16, 128), jnp.float32)
        _ctx_1024c = jax.random.dirichlet(jax.random.fold_in(_rk, 511), 0.3 * jnp.ones((16,), jnp.float32), (4, 77))
        _ctx_1024t = jnp.einsum('bsk,bkd->bsd', _ctx_1024c, _ctx_1024P)
        _ctx_1024t = _ctx_1024t * jax.lax.rsqrt(jnp.mean(jnp.square(_ctx_1024t)) + 1e-12) * 0.953939
        ctx_1024 = -1.39393e-06 + 0.999914 * (_ctx_1024t + 0.3 * jax.random.normal(jax.random.fold_in(_rk, 611), (4, 77, 128), jnp.float32))
        return (x, ctx_1024)
    x, ctx_1024 = _rec_inputs()

    def _L0_attn_setup():
        import jax, jax.numpy as jnp
        import numpy as np
        B, S, E, H, P = (2, 256, 128, 16, 256)
        HD = E // H
        key = jax.random.key(seed)
        ks = jax.random.split(key, 10)
        std = E ** (-0.5)
        x = jax.random.normal(ks[0], (B, S, E), jnp.float32)
        Wq = jax.random.normal(ks[1], (E, E), jnp.float32) * std
        Wk = jax.random.normal(ks[2], (E, E), jnp.float32) * std
        Wv = jax.random.normal(ks[3], (E, E), jnp.float32) * std
        Wo = jax.random.normal(ks[4], (E, E), jnp.float32) * std
        rel_key = jax.random.normal(ks[5], (P, HD), jnp.float32) * 0.02
        z = jnp.zeros((E,), jnp.float32)
        return {'x': x, 'Wq': Wq, 'bq': z, 'Wk': Wk, 'bk': z, 'Wv': Wv, 'bv': z, 'Wo': Wo, 'bo': z, 'rel_key': rel_key}
    _L0_attn_all = _L0_attn_setup()
    _L0_attn_in = {k: v for k, v in _L0_attn_all.items() if k in ('Wq', 'bq', 'Wk', 'bk', 'Wv', 'bv', 'Wo', 'bo', 'rel_key')}
    del _L0_attn_all

    def _L0_xattn_setup():
        import jax, jax.numpy as jnp
        import numpy as np
        NUM_HEADS = 16
        D_MODEL = 128
        HEAD_DIM = D_MODEL // NUM_HEADS
        SCALE = 8.0 / HEAD_DIM
        LN_EPS = 1e-05

        def _layernorm(x, g, b):
            mu = jnp.mean(x, axis=-1, keepdims=True)
            var = jnp.mean(jnp.square(x - mu), axis=-1, keepdims=True)
            return (x - mu) * jax.lax.rsqrt(var + LN_EPS) * g + b
        key = jax.random.key(seed)
        ks = jax.random.split(key, 8)
        B, N, M = (2, 256, 256)
        std = 1.0 / np.sqrt(D_MODEL)
        return {'x1': jax.random.normal(ks[0], (B, N, D_MODEL), jnp.float32), 'x2': jax.random.normal(ks[1], (B, M, D_MODEL), jnp.float32), 'Wq': jax.random.normal(ks[2], (D_MODEL, D_MODEL), jnp.float32) * std, 'Wk': jax.random.normal(ks[3], (D_MODEL, D_MODEL), jnp.float32) * std, 'Wv': jax.random.normal(ks[4], (D_MODEL, D_MODEL), jnp.float32) * std, 'Wp': jax.random.normal(ks[5], (D_MODEL, D_MODEL), jnp.float32) * std, 'bp': jnp.zeros((D_MODEL,), jnp.float32), 'ln_g': jnp.ones((HEAD_DIM,), jnp.float32), 'ln_b': jnp.zeros((HEAD_DIM,), jnp.float32)}
    _L0_xattn_all = _L0_xattn_setup()
    _L0_xattn_in = {k: v for k, v in _L0_xattn_all.items() if k in ('Wq', 'Wk', 'Wv', 'Wp', 'bp', 'ln_g', 'ln_b')}
    del _L0_xattn_all

    def _L0_ffn_setup():
        import jax, jax.numpy as jnp
        import numpy as np
        E = 8
        K = 2
        D = 128
        H = 128
        B, T = (2, 128)
        key = jax.random.key(seed)
        ks = jax.random.split(key, 6)
        s = 0.02
        return {'x': jax.random.normal(ks[0], (B, T, D), dtype=jnp.float32), 'gate_w': jax.random.normal(ks[1], (E, D), dtype=jnp.float32) * s, 'lb_bias': jnp.zeros((E,), dtype=jnp.float32), 'w1': jax.random.normal(ks[2], (E, H, D), dtype=jnp.float32) * s, 'w2': jax.random.normal(ks[3], (E, D, H), dtype=jnp.float32) * s, 'cfc': jax.random.normal(ks[4], (H, D), dtype=jnp.float32) * s, 'cproj': jax.random.normal(ks[5], (D, H), dtype=jnp.float32) * s}
    _L0_ffn_all = _L0_ffn_setup()
    _L0_ffn_in = {k: v for k, v in _L0_ffn_all.items() if k in ('gate_w', 'lb_bias', 'w1', 'w2', 'cfc', 'cproj')}
    del _L0_ffn_all
    return {'x': x, 'ctx_1024': ctx_1024, 'L0_attn_Wq': _L0_attn_in['Wq'], 'L0_attn_bq': _L0_attn_in['bq'], 'L0_attn_Wk': _L0_attn_in['Wk'], 'L0_attn_bk': _L0_attn_in['bk'], 'L0_attn_Wv': _L0_attn_in['Wv'], 'L0_attn_bv': _L0_attn_in['bv'], 'L0_attn_Wo': _L0_attn_in['Wo'], 'L0_attn_bo': _L0_attn_in['bo'], 'L0_attn_rel_key': _L0_attn_in['rel_key'], 'L0_xattn_Wq': _L0_xattn_in['Wq'], 'L0_xattn_Wk': _L0_xattn_in['Wk'], 'L0_xattn_Wv': _L0_xattn_in['Wv'], 'L0_xattn_Wp': _L0_xattn_in['Wp'], 'L0_xattn_bp': _L0_xattn_in['bp'], 'L0_xattn_ln_g': _L0_xattn_in['ln_g'], 'L0_xattn_ln_b': _L0_xattn_in['ln_b'], 'L0_ffn_gate_w': _L0_ffn_in['gate_w'], 'L0_ffn_lb_bias': _L0_ffn_in['lb_bias'], 'L0_ffn_w1': _L0_ffn_in['w1'], 'L0_ffn_w2': _L0_ffn_in['w2'], 'L0_ffn_cfc': _L0_ffn_in['cfc'], 'L0_ffn_cproj': _L0_ffn_in['cproj']}

def reference(x, ctx_1024, L0_attn_Wq, L0_attn_bq, L0_attn_Wk, L0_attn_bk, L0_attn_Wv, L0_attn_bv, L0_attn_Wo, L0_attn_bo, L0_attn_rel_key, L0_xattn_Wq, L0_xattn_Wk, L0_xattn_Wv, L0_xattn_Wp, L0_xattn_bp, L0_xattn_ln_g, L0_xattn_ln_b, L0_ffn_gate_w, L0_ffn_lb_bias, L0_ffn_w1, L0_ffn_w2, L0_ffn_cfc, L0_ffn_cproj):
    import jax
    import jax.numpy as jnp

    def _L0_attn_ref(x, Wq, bq, Wk, bk, Wv, bv, Wo, bo, rel_key):
        import jax, jax.numpy as jnp
        import numpy as np
        B, S, E, H, P = (2, 256, 128, 16, 256)
        HD = E // H
        b, s, e = x.shape
        p, hd = rel_key.shape
        h = e // hd
        scale = hd ** (-0.5)

        def split_heads(t):
            return t.reshape(b, s, h, hd).transpose(0, 2, 1, 3)
        q = split_heads(x @ Wq + bq)
        k = split_heads(x @ Wk + bk)
        v = split_heads(x @ Wv + bv)
        scores = jnp.einsum('bhid,bhjd->bhij', q, k)
        rel = jnp.einsum('bhid,pd->bhip', q, rel_key)
        i = jnp.arange(s)[:, None]
        j = jnp.arange(s)[None, :]
        rel_idx = jnp.clip(j - i + p - 1, 0, p - 1)
        bias = jnp.take_along_axis(rel, jnp.broadcast_to(rel_idx[None, None], (b, h, s, s)), axis=3)
        causal = j <= i
        logits = jnp.where(causal[None, None], (scores + bias) * scale, -jnp.inf)
        attn = jax.nn.softmax(logits, axis=-1)
        out = jnp.einsum('bhij,bhjd->bhid', attn, v)
        out = out.transpose(0, 2, 1, 3).reshape(b, s, e)
        return out @ Wo + bo

    def _L0_xattn_ref(x1, x2, Wq, Wk, Wv, Wp, bp, ln_g, ln_b):
        import jax, jax.numpy as jnp
        import numpy as np
        NUM_HEADS = 16
        D_MODEL = 128
        HEAD_DIM = D_MODEL // NUM_HEADS
        SCALE = 8.0 / HEAD_DIM
        LN_EPS = 1e-05

        def _layernorm(x, g, b):
            mu = jnp.mean(x, axis=-1, keepdims=True)
            var = jnp.mean(jnp.square(x - mu), axis=-1, keepdims=True)
            return (x - mu) * jax.lax.rsqrt(var + LN_EPS) * g + b
        B, N, C = x1.shape
        M = x2.shape[1]
        H, D = (NUM_HEADS, HEAD_DIM)
        q = (x1 @ Wq.T).reshape(B, N, H, D).transpose(0, 2, 1, 3)
        k = (x2 @ Wk.T).reshape(B, M, H, D).transpose(0, 2, 1, 3)
        v = (x2 @ Wv.T).reshape(B, M, H, D).transpose(0, 2, 1, 3)
        q = _layernorm(q, ln_g, ln_b)
        k = _layernorm(k, ln_g, ln_b)
        q = q * SCALE
        attn = jnp.einsum('bhnd,bhmd->bhnm', q, k)
        attn = jax.nn.softmax(attn, axis=-1)
        out = jnp.einsum('bhnm,bhmd->bhnd', attn, v)
        out = out.transpose(0, 2, 1, 3).reshape(B, N, C)
        return out @ Wp.T + bp

    def _L0_ffn_ref(x, gate_w, lb_bias, w1, w2, cfc, cproj):
        import jax, jax.numpy as jnp
        import numpy as np
        E = 8
        K = 2
        D = 128
        H = 128
        B, T = (2, 128)
        Bx, Tx, Dx = x.shape
        logits = jnp.einsum('btd,ed->bte', x, gate_w)
        _, idx = jax.lax.top_k(logits + lb_bias, K)
        sel_logits = jnp.take_along_axis(logits, idx, axis=-1)
        w = jax.nn.sigmoid(sel_logits)
        w = w / (jnp.sum(w, axis=-1, keepdims=True) + 1e-06)
        xf = x.reshape(-1, Dx)
        idxf = idx.reshape(-1, K)
        wf = w.reshape(-1, K)
        onehot = jax.nn.one_hot(idxf, E, dtype=wf.dtype)
        we = jnp.einsum('nke,nk->ne', onehot, wf)
        hidden = jnp.square(jax.nn.relu(jnp.einsum('nd,ehd->neh', xf, w1)))
        expert_out = jnp.einsum('neh,edh->ned', hidden, w2)
        moe_out = jnp.einsum('ned,ne->nd', expert_out, we).reshape(Bx, Tx, Dx)
        sh = jnp.square(jax.nn.relu(jnp.einsum('btd,hd->bth', x, cfc)))
        shared = jnp.einsum('bth,dh->btd', sh, cproj)
        return moe_out + shared
    x = x + _L0_attn_ref(_layernorm(x, axis=-1), L0_attn_Wq, L0_attn_bq, L0_attn_Wk, L0_attn_bk, L0_attn_Wv, L0_attn_bv, L0_attn_Wo, L0_attn_bo, L0_attn_rel_key)
    x = x + _L0_xattn_ref(_layernorm(x, axis=-1), ctx_1024, L0_xattn_Wq, L0_xattn_Wk, L0_xattn_Wv, L0_xattn_Wp, L0_xattn_bp, L0_xattn_ln_g, L0_xattn_ln_b)
    x = x + _L0_ffn_ref(_layernorm(x, axis=-1), L0_ffn_gate_w, L0_ffn_lb_bias, L0_ffn_w1, L0_ffn_w2, L0_ffn_cfc, L0_ffn_cproj)
    return x

_drawn_inputs = setup_inputs


def setup_inputs(seed=0):
    import zlib

    import numpy as np

    out = dict(_drawn_inputs(seed))
    spreads = {'L0_attn_bq': (0.0, 0.527),
     'L0_attn_bk': (0.0, 0.8),
     'L0_attn_bv': (0.0, 0.1),
     'L0_attn_bo': (0.0, 0.1),
     'L0_xattn_bp': (0.0, 0.1),
     'L0_xattn_ln_g': (1.0, 0.2),
     'L0_xattn_ln_b': (0.0, 0.1),
     'L0_ffn_lb_bias': (0.0, 0.8)}
    factors = {'L0_attn_rel_key': 8.0,
     'L0_ffn_gate_w': 8.0,
     'L0_ffn_w1': 7.906,
     'L0_ffn_w2': 7.249,
     'L0_ffn_cfc': 5.399,
     'L0_ffn_cproj': 4.972}
    for name, (base, spread) in spreads.items():
        noise = np.random.default_rng([zlib.crc32(name.encode()), seed]).standard_normal(out[name].shape)
        drawn = base * np.exp(spread * noise) if base else spread * noise
        out[name] = jnp.asarray(drawn.astype(out[name].dtype))
    for name, factor in factors.items():
        out[name] = (out[name] * factor).astype(out[name].dtype)
    return out
```

```python
from contextlib import ExitStack

import numpy as np

import concourse.bass as bass
from concourse import mybir

F32 = mybir.dt.float32
ALU = mybir.AluOpType
ACT = mybir.ActivationFunctionType
AX_X = mybir.AxisListType.X

B, S, D = 4, 512, 128
H, HD = 16, 8
HV = HD + 1
M = 77
E = 8
P = 256
T = 128
TB = S // T
QT = T // H
STEPS = S // (2 * QT)
BS = T // (2 * QT)
SCALE = HD ** -0.5
EPS = 1e-5
RW = P + 6 * QT
MASKED = -(2.0 ** 100)
XG = 4

PACK_A = [("ident", T), ("wq", D), ("wk", D), ("wv", D), ("bv", D), ("bq", 1), ("bk", 1),
          ("head_mask", H), ("query_mask", QT), ("rel", P)]
PACK_B = [("wo", D), ("bo", D), ("xwq", D), ("xwk", D), ("xwv", D), ("xwp", D), ("xbp", D),
          ("ln_g", D), ("ln_b", D), ("gate", E), ("lb", E), ("before", E * E),
          ("w1", (E + 1) * D), ("w2", (E + 1) * D)]


def columns(pack):
    at, out = 0, {}
    for name, width in pack:
        out[name] = (at, at + width)
        at += width
    return out, at


def build(nc, x, ctx_in, pack_a, pack_b, rel_base, out):
    cols_a, wide_a = columns(PACK_A)
    cols_b, wide_b = columns(PACK_B)
    q_dram = nc.dram_tensor("q_scratch", (B, D, T + S), F32, kind="Internal").ap()

    with ExitStack() as stack:
        def sb(name, shape):
            return stack.enter_context(nc.sbuf_tensor(name, shape, F32))

        def sem(name):
            return stack.enter_context(nc.semaphore(name))

        pa_sb = sb("pack_a_sb", [128, wide_a])
        pb_sb = sb("pack_b_sb", [128, wide_b])
        ca = {n: pa_sb[:, a:z] for n, (a, z) in cols_a.items()}
        cb = {n: pb_sb[:, a:z] for n, (a, z) in cols_b.items()}
        ident = ca["ident"]

        X = sb("X", [128, B * TB, D])
        stage = sb("stage", [128, TB, D])
        xc = sb("xc", [128, TB, D])
        sq = sb("sq", [128, TB, D])
        xnT = sb("xnT", [128, S])
        stat = sb("stat", [128, 6, TB * H])
        minus_half = sb("minus_half", [128, TB * H])
        qT = sb("qT", [128, B * S])
        kT = sb("kT", [128, B * S])
        V = sb("V", [128, B * TB, H, HV])
        V_now = sb("V_now", [128, TB, H, HV])
        rel0 = sb("rel0", [HD, P])
        rel = sb("rel_shifted", [128, RW])
        q_rep = sb("q_rep", [QT * HD, 2, H, T])
        q_blk = sb("q_blk", [128, 2, T, H])
        q_rel = sb("q_rel", [128, 2, T, H])
        prob = sb("prob", [128, 4, 2, S])
        pt_even = sb("pt_even", [128, 3, BS * 2, T])
        pt_odd = sb("pt_odd", [128, 2, BS * 2, T])
        pt_diag = sb("pt_diag", [128, 2, BS * 2, T])
        pt_full = [pt_even, pt_odd]
        neg_max = sb("neg_max", [128, 2, 2])
        o_sb = sb("o_sb", [128, H, HD])
        oT = sb("oT", [128, T])
        rec = sb("rec", [128, H])

        prob_flat = prob[:].rearrange("p a b c -> p (a b c)")
        x_prob = [prob_flat[:, i * H * M:(i + 1) * H * M].rearrange("p (h j) -> p h j", h=H)
                  for i in range(2)]
        x_pT = pt_odd[:].rearrange("p a b c -> p (a b) c")[0:M, 0:H, :]
        x_key = q_blk[:].rearrange("p a b c -> p (a b c)")[:, 0:H * M].rearrange("p (h j) -> p h j", h=H)
        scratch = pt_even[:].rearrange("p a b c -> p (a b c)")
        x_q = scratch[:, 0:512]
        x_qT = scratch[:, 512:1024]
        ctx_sb = scratch[0:M, 1024:1152]
        ctxT = scratch[:, 1152:1152 + M]
        x_k = scratch[0:M, 1280:1408]
        x_v = scratch[0:M, 1408:1408 + H * HV].rearrange("p (h d) -> p h d", h=H)
        x_max = scratch[:, 1600:1616]
        k_c = scratch[0:M, 1664:1792]
        k_sq = scratch[0:M, 1792:1920]
        k_stat = scratch[0:M, 1920:2016].rearrange("p (a b) -> p a b", a=6)
        relu = prob_flat[:, 0:1024].rearrange("p (a b) -> p a b", a=2)
        hidden = prob_flat[:, 1024:2048].rearrange("p (a b) -> p a b", a=2)
        rt = scratch[:, 2048:4096]
        r_exp, r_z, r_rank, r_sel = (rt[:, 32 * i:32 * i + 32] for i in range(4))
        r_sig, r_w, r_we = (rt[:, 32 * i:32 * i + 32] for i in range(4, 7))
        r_sum, r_inv = rt[:, 240:244], rt[:, 244:248]
        r_gt, r_eq = rt[:, 256:512], rt[:, 512:768]

        psS = stack.enter_context(nc.psum_tensor("psS", [128, 4, 512], F32))
        psT = stack.enter_context(nc.psum_tensor("psT", [128, 2, 512], F32))
        psO = stack.enter_context(nc.psum_tensor("psO", [128, 512], F32))
        psM = stack.enter_context(nc.psum_tensor("psM", [128, 512], F32))

        a_loaded, b_loaded, x_loaded = sem("a_loaded"), sem("b_loaded"), sem("x_loaded")
        rel_base_loaded, rel_loaded = sem("rel_base_loaded"), sem("rel_loaded")
        q_stored, out_stored = sem("q_stored"), sem("out_stored")
        q_rep_loaded = [sem("q_rep_loaded0"), sem("q_rep_loaded1")]
        ctx_loaded = sem("ctx_loaded")
        const_ready = sem("const_ready")
        rel0_ready = sem("rel0_ready")
        vec_step = sem("vec_step")
        ln_var = sem("ln_var")
        ln_rstd = sem("ln_rstd")
        ln_done = sem("ln_done")
        bias_added = sem("bias_added")
        transposed = sem("transposed")
        psT_read = [sem("psT_read0"), sem("psT_read1")]
        psT_ready = [sem("psT_ready0"), sem("psT_ready1")]
        q_ready, k_ready = sem("q_ready"), sem("k_ready")
        qT_ready = sem("qT_ready")
        v_ready = sem("v_ready")
        q_blk_ready, q_rel_ready = sem("q_blk_ready"), sem("q_rel_ready")
        scores_ready, max_ready = sem("scores_ready"), sem("max_ready")
        scores_read = sem("scores_read")
        psO_ready, psO_read = sem("psO_ready"), sem("psO_read")
        oT_ready, oT_copied = sem("oT_ready"), sem("oT_copied")
        y_ready, y_added = sem("y_ready"), sem("y_added")
        c_tr, c_copied, c_kv, c_v = sem("c_tr"), sem("c_copied"), sem("c_kv"), sem("c_v")
        xq_ready, hn_var, hn_rstd, hn_done = sem("xq_ready"), sem("hn_var"), sem("hn_rstd"), sem("hn_done")
        xk_tr, x_key_ready, xq_tr, xq_copied = sem("xk_tr"), sem("x_key_ready"), sem("xq_tr"), sem("xq_copied")
        xs_ready, xs_shifted, xs_exp = sem("xs_ready"), sem("xs_shifted"), sem("xs_exp")
        xn_copied = sem("xn_copied")
        x_pT_vec = sem("x_pT_vec")
        g_ready, g_exp, we_ready = sem("g_ready"), sem("g_exp"), sem("we_ready")
        h_ready, h_relu, h_sq, e_ready, e_added = sem("h_ready"), sem("h_relu"), sem("h_sq"), sem("e_ready"), sem("e_added")

        ONE = 1
        PRO = 1 + B
        UNITS = 64

        def blocks():
            return [(n, TB - 1 - n) for n in range(TB)]

        def width(blk, u):
            return (blk * BS + (5 if u in (2, 3) else u + 1)) * 2 * QT

        def units(blk):
            full = [list(range(j, min(j + 2, blk))) for j in range(0, blk, 2)]
            return full + [None]

        def unit_base():
            at, first = 0, {}
            for n, blk in blocks():
                for u in range(BS):
                    first[n, u] = at
                    at += len(units(blk))
            assert at == UNITS
            return first

        first_unit = unit_base()

        def last_unit(s):
            n, u = divmod(s % STEPS, BS)
            return first_unit[n, u] + len(units(TB - 1 - n)) - 1 - (UNITS if s < 0 else 0)

        block = stack.enter_context(nc.Block())

        @block.sync
        def _(sp):
            sp.dma_start(X[:], x.rearrange("b (t p) d -> p (b t) d", p=T)).then_inc(x_loaded, 16)
            sp.dma_start(pa_sb[:], pack_a).then_inc(a_loaded, 16)
            sp.dma_start(rel[0:72, :], rel_base).then_inc(rel_base_loaded, 16)
            sp.dma_start(pb_sb[:], pack_b).then_inc(b_loaded, 16)
            sp.wait_ge(rel0_ready, 1)
            sp.wait_ge(rel_base_loaded, 16)
            for i in range(QT):
                sp.dma_start(rel[HD * i:HD * i + HD, 1 + i:1 + i + P], rel0[:]).then_inc(rel_loaded, 16)
            with sp.Fori(0, B) as b:
                sp.wait_ge(qT_ready, b + 1 + ONE)
                sp.dma_start(q_dram[bass.ds(b, 1), :, T:T + S].rearrange("o p i -> p (o i)"),
                             qT[:, bass.ds(b * S, S)]).then_inc(q_stored, 16)
            sp.wait_ge(q_stored, 16 * B)

            def load_queries(b, first):
                q_now = q_dram[bass.ds(b, 1)]
                for n, blk in blocks():
                    if not (first and n < 2):
                        sp.wait_ge(q_rel_ready, b * TB + n + 1)
                    for i in range(QT):
                        sp.dma_start(q_rep[HD * i:HD * i + HD, n % 2, :, :],
                                     q_now[:, :, (blk + 1) * T:(blk + 2) * T]
                                     .rearrange("o (h d) i -> d (o h) i", d=HD)).then_inc(q_rep_loaded[n % 2], 16)

            load_queries(0, True)
            with sp.Fori(1, B) as b:
                load_queries(b, False)

            sp.wait_ge(y_added, B * TB + ONE)
            with sp.Fori(0, B) as b:
                sp.wait_ge(c_tr, b + ONE)
                sp.dma_start(ctx_sb, ctx_in[bass.ds(b, 1)].rearrange("o m d -> m (o d)")).then_inc(ctx_loaded, 16)

            with sp.Fori(0, B) as b:
                sp.wait_ge(e_added, (b + 1) * (E + 1) + ONE)
                sp.dma_start(out[bass.ds(b, 1)].rearrange("o (t p) d -> p (o t) d", p=T),
                             X[:, bass.ds(b * TB, TB), :]).then_inc(out_stored, 16)
            sp.wait_ge(out_stored, 16 * B)

        @block.gpsimd
        def _(pool):
            def ln_rstd_step(n):
                pool.wait_ge(ln_var, n + 1)
                nc.gpsimd.tensor_tensor(stat[:, 3, 0:TB], stat[:, 2, 0:TB], minus_half[:, 0:TB],
                                        ALU.pow).then_inc(ln_rstd, 1)

            pool.sem_inc(h_sq, ONE)
            nc.gpsimd.memset(minus_half[:], -0.5).then_inc(const_ready, 1)
            nc.gpsimd.memset(V[:, :, :, HD:HV], 1.0).then_inc(const_ready, 1)
            nc.gpsimd.memset(pt_diag[:], 0.0).then_inc(const_ready, 1)
            pool.wait_ge(const_ready, 3)
            pool.wait_ge(b_loaded, 16)
            with pool.Fori(0, B) as b:
                ln_rstd_step(b)
                nc.gpsimd.tensor_tensor(X[:, bass.ds(b * TB, TB), :], X[:, bass.ds(b * TB, TB), :],
                                        cb["bo"].unsqueeze(1).to_broadcast([128, TB, D]),
                                        ALU.add).then_inc(bias_added, 1)

            def build_queries(b, first):
                for n, blk in blocks():
                    slot = n % 2
                    if not (first and n < 2):
                        pool.wait_ge(scores_ready, b * STEPS + (n - 1) * BS)
                    nc.gpsimd.tensor_tensor(
                        q_blk[:, slot],
                        qT[:, bass.ds(b * S + blk * T, T)].unsqueeze(2).to_broadcast([128, T, H]),
                        ca["head_mask"].unsqueeze(1).to_broadcast([128, T, H]),
                        ALU.mult).then_inc(q_blk_ready, 1)
                    pool.wait_ge(q_rep_loaded[slot], (b * 2 + n // 2 + 1) * 16 * QT)
                    nc.gpsimd.tensor_tensor(
                        q_rel[0:QT * HD, slot].rearrange("p (g i) h -> p g i h", i=QT),
                        q_rep[:, slot].rearrange("p h (g i) -> p g i h", i=QT),
                        ca["query_mask"][0:QT * HD].unsqueeze(1).unsqueeze(3)
                        .to_broadcast([QT * HD, T // QT, QT, H]),
                        ALU.mult).then_inc(q_rel_ready, 1)
                    if n == 1:
                        pool.wait_ge(psO_ready, PRO + b * TB)
                        nc.gpsimd.tensor_copy(V_now[:], V[:, bass.ds(b * TB, TB)]).then_inc(v_ready, 1)

            pool.wait_ge(qT_ready, PRO)
            pool.wait_ge(psO_read, PRO)
            build_queries(0, True)
            with pool.Fori(1, B) as b:
                build_queries(b, False)

            with pool.Fori(0, B) as b:
                ln_rstd_step(b + B)
                nc.gpsimd.tensor_tensor(X[:, bass.ds(b * TB, TB), :], X[:, bass.ds(b * TB, TB), :],
                                        cb["xbp"].unsqueeze(1).to_broadcast([128, TB, D]),
                                        ALU.add).then_inc(bias_added, 1)
                for i, (st, n) in enumerate(((k_stat, H), (stat, TB * H))):
                    pool.wait_ge(hn_var, b * 2 + i + 1)
                    nc.gpsimd.tensor_tensor(st[:, 3, 0:n], st[:, 2, 0:n],
                                            minus_half[0:st.shape[0], 0:n], ALU.pow).then_inc(hn_rstd, 1)

            with pool.Fori(0, B) as b:
                ln_rstd_step(b + 2 * B)
                for e in range(E + 1):
                    pool.wait_ge(h_relu, b * (E + 1) + e + 1 + ONE)
                    if e >= 2:
                        pool.wait_ge(e_ready, b * (E + 1) + e - 1 + ONE)
                    else:
                        pool.wait_ge(e_ready, b * (E + 1) + ONE)
                    nc.gpsimd.tensor_tensor(hidden[:, e % 2], relu[:, e % 2], relu[:, e % 2],
                                            ALU.mult).then_inc(h_sq, 1)

        @block.scalar
        def _(act):
            for started in (*psT_read, scores_read, h_relu):
                act.sem_inc(started, ONE)
            act.wait_ge(a_loaded, 16)
            with act.Fori(0, B) as b:
                for half in range(2):
                    act.wait_ge(psT_ready[half], b + 1 + ONE)
                    if half == 0:
                        act.wait_ge(psO_ready, b + ONE)
                    nc.scalar.activation(xnT[:, half * 256:half * 256 + 256], psT[:, half, 0:256],
                                         ACT.Copy).then_inc(psT_read[half], 1)
                act.wait_ge(k_ready, b + 1)
                nc.scalar.activation(kT[:, bass.ds(b * S, S)], psS[:, 1, :], ACT.Identity,
                                     bias=ca["bk"]).then_inc(scores_read, 1)

            def copy_oT(k):
                act.wait_ge(oT_ready, k + 1)
                nc.scalar.activation(oT[:], psM[:, 0:T], ACT.Copy).then_inc(oT_copied, 1)

            with act.Fori(0, B) as b:
                for n, blk in blocks():
                    for u in range(BS):
                        s = n * BS + u
                        wide = width(blk, u)
                        if n and u == BS - 1:
                            copy_oT(b * TB + n - 1)
                        act.wait_ge(max_ready, b * STEPS + s + 1)
                        k = last_unit(s - 4)
                        act.wait_ge(psT_ready[k % 2], PRO + b * (UNITS // 2) + k // 2 + 1)
                        for r in range(2):
                            ins = nc.scalar.activation(prob[:, s % 4, r, 0:wide], psS[:, 2 * (s % 2) + r, 0:wide],
                                                       ACT.Exp, bias=neg_max[:, s % 2, r:r + 1])
                        ins.then_inc(scores_read, 1)
                copy_oT(b * TB + TB - 1)

            with act.Fori(0, B) as b:
                act.wait_ge(c_tr, b + 1 + ONE)
                nc.scalar.activation(ctxT, psM[:, 0:M], ACT.Copy).then_inc(c_copied, 1)
                act.wait_ge(transposed, b + 1)
                nc.scalar.activation(xnT[:], psT[:, 0, :], ACT.Copy).then_inc(xn_copied, 1)
                act.wait_ge(xq_tr, b + 1)
                nc.scalar.activation(x_qT, psT[:, 1, :], ACT.Copy).then_inc(xq_copied, 1)

                def x_exp(t):
                    act.wait_ge(xs_shifted, b * TB + t + 1)
                    nc.scalar.activation(x_prob[t % 2], x_prob[t % 2], ACT.Exp).then_inc(xs_exp, 1)

                x_exp(0)
                for t in range(TB):
                    for g in (0, 2, 3):
                        k = (b * TB + t) * 2 + g // 2
                        act.wait_ge(psT_ready[g % 2], PRO + B * UNITS // 2 + k + 1)
                        act.wait_ge(psO_ready, PRO + B * TB + b * TB + t)
                        nc.scalar.activation(x_pT[:, g * XG:g * XG + XG, :],
                                             psT[0:M, g % 2, :].rearrange("p (h i) -> p h i", h=XG),
                                             ACT.Copy).then_inc(psT_read[g % 2], 1)
                    if t:
                        copy_oT(B * TB + b * TB + t - 1)
                    if t + 1 < TB:
                        x_exp(t + 1)
                copy_oT(B * TB + b * TB + TB - 1)

            with act.Fori(0, B) as b:
                act.wait_ge(transposed, B + b + 1)
                nc.scalar.activation(xnT[:], psT[:, 0, :], ACT.Copy).then_inc(xn_copied, 1)
                act.wait_ge(g_ready, b + 1)
                nc.scalar.activation(r_exp, psM[:, 0:TB * E], ACT.Exp, scale=-1.0).then_inc(g_exp, 1)
                for e in range(E + 1):
                    act.wait_ge(h_ready, b * (E + 1) + e + 1)
                    if e >= 2:
                        act.wait_ge(h_sq, b * (E + 1) + e - 1 + ONE)
                    else:
                        act.wait_ge(h_sq, b * (E + 1) + ONE)
                    nc.scalar.activation(relu[:, e % 2], psS[:, e % 4, :], ACT.Relu).then_inc(h_relu, 1)

        @block.vector
        def _(dve):
            class Chain:

                def __init__(self):
                    self.base, self.n = 0, 0

                def loop(self, i, start, per):
                    self.base, self.n, self.per = start + i * per, 0, per

                def done(self):
                    assert self.n == self.per, self.n

                def link(self, ins):
                    self.n += 1
                    ins.then_inc(vec_step, 1)
                    dve.wait_ge(vec_step, self.base + self.n)

            c = Chain()
            LN, HN = 5, 7
            v = nc.vector

            def layer_norm(b, n):
                xt = X[:, bass.ds(b * TB, TB), :]
                c.link(v.reduce_sum(stat[:, 0, 0:TB], xt, AX_X))
                c.link(v.tensor_scalar(stat[:, 4, 0:TB], stat[:, 0, 0:TB], 1.0 / D, None, ALU.mult))
                c.link(v.tensor_tensor(xc[:], xt, stat[:, 4, 0:TB].unsqueeze(2).to_broadcast([128, TB, D]),
                                       ALU.subtract))
                c.link(v.tensor_tensor(sq[:], xc[:], xc[:], ALU.mult))
                c.link(v.reduce_sum(stat[:, 1, 0:TB], sq[:], AX_X))
                v.tensor_scalar(stat[:, 2, 0:TB], stat[:, 1, 0:TB], 1.0 / D, EPS,
                                ALU.mult, ALU.add).then_inc(ln_var, 1)
                dve.wait_ge(ln_rstd, n + 1)
                v.tensor_tensor(stage[:], xc[:], stat[:, 3, 0:TB].unsqueeze(2).to_broadcast([128, TB, D]),
                                ALU.mult).then_inc(ln_done, 1)

            for started in (qT_ready, psO_read, y_added, e_added):
                dve.sem_inc(started, ONE)
            dve.wait_ge(a_loaded, 16)
            for slot in range(2):
                rows = slice(QT * HD, QT * HD + QT)
                v.tensor_copy(
                    q_rel[rows, slot].rearrange("p (g i) h -> p g i h", i=QT),
                    ca["query_mask"][rows].unsqueeze(1).unsqueeze(3).to_broadcast([QT, T // QT, QT, H]),
                ).then_inc(q_rel_ready, 1)
            v.tensor_scalar(rel0[:], ca["rel"][0:HD, :], ca["rel"][0:HD, 0:1], None,
                            ALU.subtract).then_inc(rel0_ready, 1)
            dve.wait_ge(x_loaded, 16)
            with dve.Fori(0, B) as b:
                c.loop(b, 0, LN)
                layer_norm(b, b)
                dve.wait_ge(q_ready, b + 1)
                v.tensor_scalar(qT[:, bass.ds(b * S, S)], psS[:, 0, :], ca["bq"], SCALE,
                                ALU.add, ALU.mult).then_inc(qT_ready, 1)
                dve.wait_ge(psO_ready, b + 1 + ONE)
                v.tensor_tensor(V[:, bass.ds(b * TB, TB), :, 0:HD].rearrange("p t h d -> p t h d"),
                                psO[:].rearrange("p (t h d) -> p t h d", t=TB, h=H),
                                ca["bv"].rearrange("p (h d) -> p h d", h=H).unsqueeze(1)
                                .to_broadcast([128, TB, H, HD]), ALU.add).then_inc(psO_read, 1)
                c.done()

            def normalise(k):
                dve.wait_ge(psO_ready, PRO + k + 1)
                o = psO[:, 0:H * HV].rearrange("p (h d) -> p h d", h=H)
                c.link(v.reciprocal(rec[:].unsqueeze(2), o[:, :, HD:HV]))
                v.tensor_tensor(o_sb[:], o[:, :, 0:HD], rec[:].unsqueeze(2).to_broadcast([128, H, HD]),
                                ALU.mult).then_inc(psO_read, 1)

            def add_y(k, tile):
                dve.wait_ge(y_ready, k + 1)
                xt = X[:, bass.ds(tile, 1), :].rearrange("p o d -> p (o d)")
                v.tensor_tensor(xt, psM[:, T:2 * T], xt, ALU.add).then_inc(y_added, 1)

            dve.wait_ge(bias_added, B)
            dve.wait_ge(const_ready, 3)
            with dve.Fori(0, B) as b:
                c.loop(b, LN * B, TB)

                def copy_units(s):
                    n, u = divmod(s, BS)
                    blk = TB - 1 - n
                    if u == 0:
                        dve.wait_ge(psO_ready, PRO + b * TB + n - 1)
                    for i, js in enumerate(units(blk)):
                        k = first_unit[n, u] + i
                        dve.wait_ge(psT_ready[k % 2], PRO + b * (UNITS // 2) + k // 2 + 1)
                        if js is None:
                            w = width(0, u)
                            dst = pt_diag[0:w, n % 2, 2 * u:2 * u + 2, :]
                            src = psT[0:w, k % 2, 0:256].rearrange("p (t m) -> p t m", t=2)
                        else:
                            dst = pt_full[n % 2][:, js[0]:js[-1] + 1, 2 * u:2 * u + 2, :]
                            src = psT[:, k % 2, 0:256 * len(js)].rearrange("p (j t m) -> p j t m", t=2, m=T)
                        v.tensor_copy(dst, src).then_inc(psT_read[k % 2], 1)

                for n, blk in blocks():
                    for u in range(BS):
                        s = n * BS + u
                        wide = width(blk, u)
                        if n and u == BS - 2:
                            normalise(b * TB + n - 1)
                        if n > 1 and u == 0:
                            add_y(b * TB + n - 2, b * TB + TB - 1 - (n - 2))
                        dve.wait_ge(scores_ready, b * STEPS + s + 1)
                        v.tensor_reduce(neg_max[:, s % 2], psS[:, 2 * (s % 2):2 * (s % 2) + 2, 0:wide],
                                        AX_X, ALU.max, negate=True).then_inc(max_ready, 1)
                        if s >= 2:
                            copy_units(s - 2)
                add_y(b * TB + TB - 2, b * TB + 1)
                copy_units(STEPS - 2)
                copy_units(STEPS - 1)
                normalise(b * TB + TB - 1)
                add_y(b * TB + TB - 1, b * TB)
                c.done()

            def head_norm(src, dst, xc_, sq_, st, parts, groups, k):
                def heads(ap):
                    return ap.rearrange("p (g d) -> p g d", d=HD)

                def spread(row):
                    return st[:, row, 0:groups].unsqueeze(2).to_broadcast([parts, groups, HD])

                c.link(v.reduce_sum(st[:, 0, 0:groups], heads(src), AX_X))
                c.link(v.tensor_scalar(st[:, 4, 0:groups], st[:, 0, 0:groups], 1.0 / HD, None, ALU.mult))
                c.link(v.tensor_tensor(heads(xc_), heads(src), spread(4), ALU.subtract))
                c.link(v.tensor_tensor(sq_, xc_, xc_, ALU.mult))
                c.link(v.reduce_sum(st[:, 1, 0:groups], heads(sq_), AX_X))
                v.tensor_scalar(st[:, 2, 0:groups], st[:, 1, 0:groups], 1.0 / HD, EPS,
                                ALU.mult, ALU.add).then_inc(hn_var, 1)
                dve.wait_ge(hn_rstd, k + 1)
                tiles = groups // H

                def tiled(ap):
                    return ap.rearrange("p (t f) -> p t f", t=tiles)

                c.link(v.tensor_tensor(heads(sq_), heads(xc_), spread(3), ALU.mult))
                c.link(v.tensor_tensor(tiled(xc_), tiled(sq_),
                                       cb["ln_g"][0:parts].unsqueeze(1).to_broadcast([parts, tiles, D]), ALU.mult))
                v.tensor_tensor(tiled(dst), tiled(xc_),
                                cb["ln_b"][0:parts].unsqueeze(1).to_broadcast([parts, tiles, D]),
                                ALU.add).then_inc(hn_done, 1)

            v.memset(x_v[:, :, HD:HV], 1.0)
            with dve.Fori(0, B) as b:
                c.loop(b, LN * B + TB * B, LN + 2 * HN + 2 * TB)
                layer_norm(b, b + B)
                dve.wait_ge(bias_added, B + b + 1)
                dve.wait_ge(c_kv, b + 1)
                v.tensor_copy(x_v[:, :, 0:HD], psS[0:M, 2, 0:D].rearrange("p (h d) -> p h d", h=H)).then_inc(c_v, 1)
                head_norm(psS[0:M, 1, 0:D], x_k, k_c, k_sq, k_stat, M, H, b * 2)
                dve.wait_ge(xq_ready, b + 1)
                head_norm(psS[:, 0, :], x_q, xc[:].rearrange("p t d -> p (t d)"),
                          sq[:].rearrange("p t d -> p (t d)"), stat, 128, TB * H, b * 2 + 1)
                dve.wait_ge(xk_tr, b + 1)
                v.tensor_tensor(x_key, psM[:, T:T + M].unsqueeze(1).to_broadcast([128, H, M]),
                                ca["head_mask"].unsqueeze(2).to_broadcast([128, H, M]),
                                ALU.mult).then_inc(x_key_ready, 1)

                def shift(t):
                    dve.wait_ge(xs_ready, b * TB + t + 1)
                    sc = psS[:, :, 0:XG * M].rearrange("p g (h j) -> p g h j", h=XG)
                    c.link(v.tensor_reduce(x_max, sc, AX_X, ALU.max, negate=True))
                    v.tensor_tensor(x_prob[t % 2].rearrange("p (g h) j -> p g h j", h=XG), sc,
                                    x_max.rearrange("p (g h) -> p g h", h=XG).unsqueeze(3)
                                    .to_broadcast([128, H // XG, XG, M]), ALU.add).then_inc(xs_shifted, 1)

                shift(0)
                for t in range(TB):
                    k = B * TB + b * TB + t
                    if t + 1 < TB:
                        shift(t + 1)
                    dve.wait_ge(psT_ready[1], PRO + B * UNITS // 2 + (b * TB + t) * 2 + 1)
                    v.tensor_copy(x_pT[:, XG:2 * XG, :],
                                  psT[0:M, 1, :].rearrange("p (h i) -> p h i", h=XG)).then_inc(psT_read[1], 1)
                    if t:
                        add_y(k - 1, b * TB + t - 1)
                    normalise(k)
                add_y(B * TB + b * TB + TB - 1, b * TB + TB - 1)
                c.done()

            with dve.Fori(0, B) as b:
                c.loop(b, LN * B + TB * B + (LN + 2 * HN + 2 * TB) * B, LN + 11)
                layer_norm(b, b + 2 * B)
                dve.wait_ge(g_exp, b + 1)
                c.link(v.tensor_tensor(r_z.rearrange("p (t e) -> p t e", t=TB),
                                       psM[:, 0:TB * E].rearrange("p (t e) -> p t e", t=TB),
                                       cb["lb"].unsqueeze(1).to_broadcast([128, TB, E]), ALU.add))
                mine = r_z.unsqueeze(2).to_broadcast([128, TB * E, E])
                other = r_z.rearrange("p (t e) -> p t e", t=TB).unsqueeze(2).to_broadcast([128, TB, E, E])
                mine4 = mine.rearrange("p (t e) f -> p t e f", t=TB)
                c.link(v.tensor_tensor(r_gt.rearrange("p (t e f) -> p t e f", t=TB, e=E), mine4, other, ALU.is_lt))
                c.link(v.tensor_tensor(r_eq.rearrange("p (t e f) -> p t e f", t=TB, e=E), mine4, other, ALU.is_equal))
                before = cb["before"].unsqueeze(1).to_broadcast([128, TB, E * E])
                eq = r_eq.rearrange("p (t f) -> p t f", t=TB)
                c.link(v.tensor_tensor(eq, eq, before, ALU.mult))
                c.link(v.tensor_tensor(r_gt, r_gt, r_eq, ALU.add))
                c.link(v.reduce_sum(r_rank, r_gt.rearrange("p (g f) -> p g f", f=E), AX_X))
                c.link(v.tensor_scalar(r_sig, r_exp, 1.0, None, ALU.add))
                c.link(v.reciprocal(r_sig, r_sig))
                c.link(v.scalar_tensor_tensor(out=r_w, in0=r_rank, scalar=2.0, in1=r_sig,
                                              op0=ALU.is_lt, op1=ALU.mult))
                w3 = r_w.rearrange("p (t e) -> p t e", t=TB)
                c.link(v.reduce_sum(r_sum, w3, AX_X))
                c.link(v.tensor_scalar(r_sum, r_sum, 1e-6, None, ALU.add))
                v.reciprocal(r_inv, r_sum).then_inc(we_ready, 1)
                dve.wait_ge(we_ready, 2 * b + 1)
                v.tensor_tensor(r_we.rearrange("p (t e) -> p t e", t=TB), w3,
                                r_inv.unsqueeze(2).to_broadcast([128, TB, E]), ALU.mult).then_inc(we_ready, 1)
                dve.wait_ge(we_ready, 2 * b + 2)
                for e in range(E + 1):
                    dve.wait_ge(e_ready, b * (E + 1) + e + 1 + ONE)
                    dve.wait_ge(e_added, b * (E + 1) + e + ONE)
                    if e == E:
                        xt = X[:, bass.ds(b * TB, TB), :]
                        v.tensor_tensor(xt, psT[:, e % 2, :].rearrange("p (t d) -> p t d", t=TB), xt,
                                        ALU.add).then_inc(e_added, 1)
                        continue
                    for t in range(TB):
                        xt = X[:, bass.ds(b * TB + t, 1), :].rearrange("p o d -> p (o d)")
                        ins = v.scalar_tensor_tensor(out=xt, in0=psT[:, e % 2, t * T:t * T + T],
                                                     scalar=r_we[:, t * E + e:t * E + e + 1], in1=xt,
                                                     op0=ALU.mult, op1=ALU.add)
                    ins.then_inc(e_added, 1)
                c.done()

        @block.tensor
        def _(pe):
            mm = nc.tensor.matmul

            for started in (*psT_ready, psO_ready, c_tr, e_ready):
                pe.sem_inc(started, ONE)
            pe.wait_ge(a_loaded, 16)
            with pe.Fori(0, B) as b:
                pe.wait_ge(ln_done, b + 1)
                for half in range(2):
                    pe.wait_ge(psT_read[half], b + ONE)
                    for i in range(2):
                        ins = nc.tensor.transpose(psT[:, half, i * T:i * T + T], stage[:, 2 * half + i, :], ident)
                    ins.then_inc(psT_ready[half], 1)
                for half in range(2):
                    pe.wait_ge(psT_read[half], b + 1 + ONE)
                pe.wait_ge(qT_ready, b + ONE)
                mm(psS[:, 0, :], ca["wq"], xnT[:], start=True, stop=True).then_inc(q_ready, 1)
                pe.wait_ge(scores_read, b + ONE)
                mm(psS[:, 1, :], ca["wk"], xnT[:], start=True, stop=True).then_inc(k_ready, 1)
                pe.wait_ge(psO_read, b + ONE)
                for t in range(TB):
                    ins = mm(psO[:, t * D:t * D + D], xnT[:, t * T:t * T + T], ca["wv"], start=True, stop=True)
                ins.then_inc(psO_ready, 1)

            def attend(k, b, n, heads, v_of, last):
                for h in heads:
                    parts = v_of(h)
                    for i, (w, val) in enumerate(parts):
                        ins = mm(psO[:, h * HV:h * HV + HV], w, val, start=(i == 0), stop=(i == len(parts) - 1))
                if last:
                    ins.then_inc(psO_ready, 1)

            def transpose_o(k):
                pe.wait_ge(psO_read, PRO + k + 1)
                pe.wait_ge(y_added, k + ONE)
                nc.tensor.transpose(psM[:, 0:T], o_sb[:].rearrange("p h d -> p (h d)"), ident).then_inc(oT_ready, 1)

            def project_o(k, w):
                pe.wait_ge(oT_copied, k + 1)
                mm(psM[:, T:2 * T], oT[:], w, start=True, stop=True).then_inc(y_ready, 1)

            pe.wait_ge(rel_loaded, 16 * QT)
            pe.wait_ge(b_loaded, 16)
            pe.wait_ge(qT_ready, PRO)
            pe.wait_ge(psO_read, PRO)
            pe.wait_ge(scores_read, PRO)
            with pe.Fori(0, B) as b:
                def scores(s):
                    n, u = divmod(s, BS)
                    blk = TB - 1 - n
                    wide = width(blk, u)
                    if u == 0:
                        pe.wait_ge(q_blk_ready, b * TB + n + 1)
                        pe.wait_ge(q_rel_ready, b * TB + n + 3)
                    pe.wait_ge(scores_read, PRO + b * STEPS + s - 1)
                    for r in range(2):
                        q0 = (2 * u + r) * QT
                        i0 = blk * T + q0
                        lo = max(0, i0 - P)
                        dst = psS[:, 2 * (s % 2) + r, :]
                        mm(dst[:, 0:wide], q_blk[:, n % 2, q0:q0 + QT, :].rearrange("p i h -> p (i h)"),
                           kT[:, bass.ds(b * S, wide)], start=True, stop=False)
                        ins = mm(dst[:, lo:wide],
                                 q_rel[0:QT * HD + QT, n % 2, q0:q0 + QT, :].rearrange("p i h -> p (i h)"),
                                 rel[0:QT * HD + QT, lo - i0 + P:wide - i0 + P], start=False, stop=True)
                    ins.then_inc(scores_ready, 1)

                def transpose_weights(s):
                    n, u = divmod(s, BS)
                    blk = TB - 1 - n
                    pe.wait_ge(scores_read, PRO + b * STEPS + s + 1)
                    for i, js in enumerate(units(blk)):
                        k = first_unit[n, u] + i
                        pe.wait_ge(psT_read[k % 2], PRO + b * (UNITS // 2) + k // 2)
                        w = T if js else width(0, u)
                        for jn, j in enumerate(js or [blk]):
                            for r in range(2):
                                at = (jn * 2 + r) * T
                                ins = nc.tensor.transpose(psT[0:w, k % 2, at:at + T],
                                                          prob[:, s % 4, r, j * T:j * T + w], ident)
                        ins.then_inc(psT_ready[k % 2], 1)

                def copied(n):
                    last = first_unit[n, BS - 1] + len(units(TB - 1 - n)) - 1
                    for k in (last - 1, last):
                        pe.wait_ge(psT_read[k % 2], PRO + b * (UNITS // 2) + k // 2 + 1)

                def attend_block(n, heads):
                    blk = TB - 1 - n
                    k = b * TB + n
                    if heads[0] == 0:
                        if n == 0:
                            pe.wait_ge(v_ready, b + 1)
                        copied(n)
                        pe.wait_ge(psO_read, PRO + k)

                    def parts(h):
                        def w(buf):
                            return buf.rearrange("p t (i h) -> p (t i) h", h=H)[:, :, h]
                        return [(w(pt_full[n % 2][:, j]), V_now[:, j, h, :]) for j in range(blk)] + \
                               [(w(pt_diag[:, n % 2]), V_now[:, blk, h, :])]

                    attend(k, b, n, heads, parts, heads[-1] == H - 1)

                for s in range(STEPS):
                    n, u = divmod(s, BS)
                    scores(s)
                    if s >= 2:
                        transpose_weights(s - 2)
                    if n and 2 <= u <= 5:
                        attend_block(n - 1, range(4 * (u - 2), 4 * (u - 2) + 4))
                    if n and u == 6:
                        transpose_o(b * TB + n - 1)
                    if n and u == 7:
                        project_o(b * TB + n - 1, cb["wo"])
                transpose_weights(STEPS - 2)
                transpose_weights(STEPS - 1)
                attend_block(TB - 1, range(H))
                transpose_o(b * TB + TB - 1)
                project_o(b * TB + TB - 1, cb["wo"])

            pe.wait_ge(y_added, B * TB + ONE)
            with pe.Fori(0, B) as b:
                pe.wait_ge(ctx_loaded, 16 * (b + 1))
                pe.wait_ge(y_added, B * TB + b * TB + ONE)
                nc.tensor.transpose(psM[:, 0:M], ctx_sb, ident[0:M, 0:M]).then_inc(c_tr, 1)
                pe.wait_ge(ln_done, B + b + 1)
                for j in range(2):
                    pe.wait_ge(psT_read[j], PRO + B * UNITS // 2 + b * 2 * TB)
                for t in range(TB):
                    ins = nc.tensor.transpose(psT[:, 0, t * T:t * T + T], stage[:, t, :], ident)
                ins.then_inc(transposed, 1)
                pe.wait_ge(c_copied, b + 1)
                mm(psS[0:M, 1, 0:D], ctxT, cb["xwk"], start=True, stop=True)
                mm(psS[0:M, 2, 0:D], ctxT, cb["xwv"], start=True, stop=True).then_inc(c_kv, 1)
                pe.wait_ge(xn_copied, b + 1)
                for t in range(TB):
                    ins = mm(psS[:, 0, t * D:t * D + D], xnT[:, t * T:t * T + T], cb["xwq"], start=True, stop=True)
                ins.then_inc(xq_ready, 1)
                pe.wait_ge(hn_done, b * 2 + 1)
                nc.tensor.transpose(psM[:, T:T + M], x_k, ident[0:M, 0:M]).then_inc(xk_tr, 1)
                pe.wait_ge(hn_done, b * 2 + 2)
                for t in range(TB):
                    ins = nc.tensor.transpose(psT[:, 1, t * T:t * T + T], x_q[:, t * T:t * T + T], ident)
                ins.then_inc(xq_tr, 1)
                pe.wait_ge(xq_copied, b + 1)
                pe.wait_ge(x_key_ready, b + 1)
                pe.wait_ge(c_v, b + 1)

                def x_scores(t):
                    if t:
                        pe.wait_ge(xs_shifted, b * TB + t)
                    for g in range(H // XG):
                        ins = mm(psS[:, g, 0:XG * M], x_qT[:, t * T:t * T + T],
                                 x_key[:, g * XG:g * XG + XG, :].rearrange("p h j -> p (h j)"),
                                 start=True, stop=True)
                    ins.then_inc(xs_ready, 1)

                x_scores(0)
                for t in range(TB):
                    k = B * TB + b * TB + t
                    if t + 1 < TB:
                        x_scores(t + 1)
                    pe.wait_ge(xs_exp, b * TB + t + 1)
                    for g in range(H // XG):
                        m = (b * TB + t) * 2 + g // 2
                        pe.wait_ge(psT_read[g % 2], PRO + B * UNITS // 2 + m)
                        for i in range(XG):
                            ins = nc.tensor.transpose(psT[0:M, g % 2, i * T:i * T + T],
                                                      x_prob[t % 2][:, g * XG + i, :], ident)
                        ins.then_inc(psT_ready[g % 2], 1)
                    if t:
                        transpose_o(k - 1)
                    for j in range(2):
                        pe.wait_ge(psT_read[j], PRO + B * UNITS // 2 + (b * TB + t) * 2 + 2)
                    pe.wait_ge(psO_read, PRO + k)
                    attend(k, b, 0, range(H), lambda h: [(x_pT[:, h, :], x_v[:, h, :])], True)
                    if t:
                        project_o(k - 1, cb["xwp"])
                transpose_o(B * TB + b * TB + TB - 1)
                project_o(B * TB + b * TB + TB - 1, cb["xwp"])

            pe.wait_ge(y_added, 2 * B * TB + ONE)
            with pe.Fori(0, B) as b:
                pe.wait_ge(ln_done, 2 * B + b + 1)
                pe.wait_ge(e_added, b * (E + 1) + ONE)
                for t in range(TB):
                    ins = nc.tensor.transpose(psT[:, 0, t * T:t * T + T], stage[:, t, :], ident)
                ins.then_inc(transposed, 1)
                pe.wait_ge(xn_copied, B + b + 1)
                for t in range(TB):
                    ins = mm(psM[:, t * E:t * E + E], xnT[:, t * T:t * T + T], cb["gate"], start=True, stop=True)
                ins.then_inc(g_ready, 1)

                def up(e):
                    pe.wait_ge(h_relu, b * (E + 1) + max(e - 3, 0) + ONE)
                    mm(psS[:, e % 4, :], cb["w1"][:, e * D:e * D + D], xnT[:], start=True, stop=True)\
                        .then_inc(h_ready, 1)

                up(0)
                up(1)
                for e in range(E + 1):
                    if e + 2 < E + 1:
                        up(e + 2)
                    pe.wait_ge(h_sq, b * (E + 1) + e + 1 + ONE)
                    pe.wait_ge(e_added, b * (E + 1) + max(e - 1, 0) + ONE)
                    for t in range(TB):
                        ins = mm(psT[:, e % 2, t * D:t * D + D], hidden[:, e % 2, t * T:t * T + T],
                                 cb["w2"][:, e * D:e * D + D], start=True, stop=True)
                    ins.then_inc(e_ready, 1)


def pack(parts, spec):
    width = sum(w for _, w in spec)
    out, at = np.zeros((128, width), np.float32), 0
    for name, w in spec:
        a = parts[name]
        out[0:a.shape[0], at:at + w] = a
        at += w
    return out


def kernel(**inputs):
    import concourse.bacc as bacc
    from concourse.bass_utils import run_bass_kernel_spmd

    a = {n: np.asarray(v) for n, v in inputs.items()}

    def rows(v):
        return np.broadcast_to(v.reshape(1, -1), (128, v.size))

    part = np.arange(128)
    head_mask = (part[:, None] // HD == np.arange(H)[None, :]).astype(np.float32)
    query_mask = np.zeros((128, QT), np.float32)
    query_mask[:QT * HD] = part[:QT * HD, None] // HD == np.arange(QT)[None, :]
    query_mask[QT * HD:QT * HD + QT] = np.eye(QT)
    before = np.broadcast_to((np.arange(E)[None, :] < np.arange(E)[:, None]).astype(np.float32).reshape(1, -1),
                             (128, E * E))
    rel_base = np.zeros((72, RW), np.float32)
    ahead = np.arange(RW)[None, :] - P - np.arange(QT)[:, None] > 0
    rel_base[QT * HD:] = np.where(ahead, np.float32(MASKED), np.float32(0.0))

    pack_a = pack({
        "ident": np.eye(128, dtype=np.float32), "wq": a["L0_attn_Wq"], "wk": a["L0_attn_Wk"],
        "wv": a["L0_attn_Wv"], "bv": rows(a["L0_attn_bv"]), "bq": a["L0_attn_bq"].reshape(D, 1),
        "bk": a["L0_attn_bk"].reshape(D, 1), "head_mask": head_mask, "query_mask": query_mask,
        "rel": a["L0_attn_rel_key"].T}, PACK_A)
    pack_b = pack({
        "wo": a["L0_attn_Wo"], "bo": rows(a["L0_attn_bo"]), "xwq": a["L0_xattn_Wq"].T,
        "xwk": a["L0_xattn_Wk"].T, "xwv": a["L0_xattn_Wv"].T, "xwp": a["L0_xattn_Wp"].T,
        "xbp": rows(a["L0_xattn_bp"]), "ln_g": rows(np.tile(a["L0_xattn_ln_g"], H)),
        "ln_b": rows(np.tile(a["L0_xattn_ln_b"], H)), "gate": a["L0_ffn_gate_w"].T,
        "lb": rows(a["L0_ffn_lb_bias"]), "before": before,
        "w1": np.concatenate([w.T for w in a["L0_ffn_w1"]] + [a["L0_ffn_cfc"].T], axis=1),
        "w2": np.concatenate([w.T for w in a["L0_ffn_w2"]] + [a["L0_ffn_cproj"].T], axis=1)}, PACK_B)

    nc = bacc.Bacc("TRN2", target_bir_lowering=False, num_devices=1)
    arrays = {"x": a["x"], "ctx": a["ctx_1024"], "pack_a": pack_a, "pack_b": pack_b, "rel_base": rel_base}
    arrays = {n: np.ascontiguousarray(v) for n, v in arrays.items()}
    aps = [nc.dram_tensor(n + "_dram", v.shape, mybir.dt.from_np(v.dtype), kind="ExternalInput").ap()
           for n, v in arrays.items()]
    out = nc.dram_tensor("out_dram", (B, S, D), F32, kind="ExternalOutput").ap()
    build(nc, *aps, out)
    r = run_bass_kernel_spmd(nc, [{n + "_dram": v for n, v in arrays.items()}], core_ids=[0])
    return r.results[0]["out_dram"]
```

```python
from contextlib import ExitStack

import numpy as np

import concourse.bass as bass
from concourse import mybir

F32 = mybir.dt.float32
ALU = mybir.AluOpType
ACT = mybir.ActivationFunctionType
AX_X = mybir.AxisListType.X

B, S, D = 4, 512, 128
H, HD = 16, 8
HQ = 4
M = 77
E = 8
P = 256
T = 128
TB = S // T
QT = T // H
STEPS = S // (2 * QT)
BS = T // (2 * QT)
SCALE = HD ** -0.5
EPS = 1e-5
RW = P + 6 * QT
MASKED = -(2.0 ** 100)
XG = 4

PACK_A = [("ident", T), ("wq", D), ("wk", D), ("wv", D), ("bv", D), ("bq", 1), ("bk", 1),
          ("head_mask", H), ("query_mask", QT), ("rel", P), ("row_query", QT), ("row_head", D)]
PACK_B = [("wo", D), ("bo", D), ("xwq", D), ("xwk", D), ("xwv", D), ("xwp", D), ("xbp", D),
          ("ln_g", D), ("ln_b", D), ("gate", E), ("lb", E), ("before", E * E),
          ("w1", (E + 1) * D), ("w2", (E + 1) * D)]


def columns(pack):
    at, out = 0, {}
    for name, width in pack:
        out[name] = (at, at + width)
        at += width
    return out, at


def build(nc, x, ctx_in, pack_a, pack_b, rel_base, out):
    cols_a, wide_a = columns(PACK_A)
    cols_b, wide_b = columns(PACK_B)
    q_dram = nc.dram_tensor("q_scratch", (B, D, T + S), F32, kind="Internal").ap()

    with ExitStack() as stack:
        def sb(name, shape):
            return stack.enter_context(nc.sbuf_tensor(name, shape, F32))

        def sem(name):
            return stack.enter_context(nc.semaphore(name))

        pa_sb = sb("pack_a_sb", [128, wide_a])
        pb_sb = sb("pack_b_sb", [128, wide_b])
        ca = {n: pa_sb[:, a:z] for n, (a, z) in cols_a.items()}
        cb = {n: pb_sb[:, a:z] for n, (a, z) in cols_b.items()}
        ident = ca["ident"]

        X = sb("X", [128, B * TB, D])
        stage = sb("stage", [128, TB, D])
        xc = sb("xc", [128, TB, D])
        sq = sb("sq", [128, TB, D])
        xnT = sb("xnT", [128, S])
        stat = sb("stat", [128, 6, TB * H])
        qT = sb("qT", [128, B * S])
        kT = sb("kT", [128, B * S])
        V = sb("V", [128, B * TB, H, HD])
        V_now = sb("V_now", [128, TB, H, HQ * HD])
        rel0 = sb("rel0", [HD, P])
        rel = sb("rel_shifted", [128, RW])
        q_rep = sb("q_rep", [QT * HD, 2, H, T])
        q_blk = sb("q_blk", [128, 2, T, H])
        q_rel = sb("q_rel", [128, 2, T, H])
        prob = sb("prob", [128, 4, 2, S])
        pt_even = sb("pt_even", [128, 3, H, T])
        pt_odd = sb("pt_odd", [128, 2, H, T])
        pt_diag = sb("pt_diag", [128, 2, H, T])
        pt_full = [pt_even, pt_odd]
        neg_max = sb("neg_max", [128, 2, 2])
        row_sum = sb("row_sum", [128, 2, 2 * BS])
        spread = sb("spread", [128, T])
        oT = sb("oT", [128, T])
        rec = sb("rec", [128, T])

        prob_flat = prob[:].rearrange("p a b c -> p (a b c)")
        x_prob = [prob_flat[:, i * H * M:(i + 1) * H * M].rearrange("p (h j) -> p h j", h=H)
                  for i in range(2)]
        x_pT = pt_odd[:].rearrange("p a b c -> p (a b) c")[0:M, 0:H, :]
        x_key = q_blk[:].rearrange("p a b c -> p (a b c)")[:, 0:H * M].rearrange("p (h j) -> p h j", h=H)
        scratch = pt_even[:].rearrange("p a b c -> p (a b c)")
        names, at = {}, 0
        for name, rows, width in (("x_q", 128, 512), ("x_qT", 128, 512), ("x_q2", 128, 512), ("ctx", M, 512),
                                  ("ctxT", 128, B * M), ("x_k", M, 512), ("k_c", M, 512), ("k_sq", M, 512),
                                  ("khT", 128, B * M), ("k_stat", M, 384), ("x_max", 128, H), ("x_sum", 128, H)):
            names[name] = scratch[0:rows, at:at + width]
            at += width
        x_q, x_qT, x_q2, ctxT, x_k, k_c, k_sq, khT, x_max, x_sum = (
            names[n] for n in ("x_q", "x_qT", "x_q2", "ctxT", "x_k", "k_c", "k_sq", "khT", "x_max", "x_sum"))
        ctx_sb = names["ctx"].rearrange("p (b d) -> p b d", b=B)
        k_stat = names["k_stat"].rearrange("p (a b) -> p a b", a=6)
        x_v_all = pt_diag[:].rearrange("p a h i -> p (a h i)")[0:M, 0:2048].rearrange("p (b h c) -> p b h c", b=B, h=H)
        x_v = pt_diag[:].rearrange("p a h i -> p (a h i)")[0:M, 2048:2560].rearrange("p (h c) -> p h c", h=H)
        relu = prob_flat[:, 0:1024].rearrange("p (a b) -> p a b", a=2)
        hidden = prob_flat[:, 1024:2048].rearrange("p (a b) -> p a b", a=2)
        rt = scratch[:, 5120:6144]
        r_exp, r_z, r_rank, r_sel = (rt[:, 32 * i:32 * i + 32] for i in range(4))
        r_sig, r_w, r_we = (rt[:, 32 * i:32 * i + 32] for i in range(4, 7))
        r_sum, r_inv = rt[:, 240:244], rt[:, 244:248]
        r_gt, r_eq = rt[:, 256:512], rt[:, 512:768]

        psS = stack.enter_context(nc.psum_tensor("psS", [128, 4, 512], F32))
        psT = stack.enter_context(nc.psum_tensor("psT", [128, 2, 512], F32))
        psO = stack.enter_context(nc.psum_tensor("psO", [128, 512], F32))
        psM = stack.enter_context(nc.psum_tensor("psM", [128, 512], F32))

        a_loaded, b_loaded, x_loaded = sem("a_loaded"), sem("b_loaded"), sem("x_loaded")
        rel_base_loaded, rel_loaded = sem("rel_base_loaded"), sem("rel_loaded")
        q_stored, out_stored = sem("q_stored"), sem("out_stored")
        q_rep_loaded = [sem("q_rep_loaded0"), sem("q_rep_loaded1")]
        ctx_loaded = sem("ctx_loaded")
        const_ready = sem("const_ready")
        rel0_ready = sem("rel0_ready")
        vec_step = sem("vec_step")
        ln_var = sem("ln_var")
        seed_log = sem("seed_log")
        seeded = sem("seeded")
        ln_done = sem("ln_done")
        bias_added = sem("bias_added")
        transposed = sem("transposed")
        psT_read = [sem("psT_read0"), sem("psT_read1")]
        psT_ready = [sem("psT_ready0"), sem("psT_ready1")]
        q_ready, k_ready = sem("q_ready"), sem("k_ready")
        qT_ready = sem("qT_ready")
        v_ready = sem("v_ready")
        q_blk_ready, q_rel_ready = sem("q_blk_ready"), sem("q_rel_ready")
        scores_ready, max_ready = sem("scores_ready"), sem("max_ready")
        scores_read = sem("scores_read")
        psO_ready, psO_read = sem("psO_ready"), sem("psO_read")
        spread_ready, sums_ready = sem("spread_ready"), sem("sums_ready")
        y_ready, y_added = sem("y_ready"), sem("y_added")
        c_tr, c_copied, c_kv, x_v_all_ready = sem("c_tr"), sem("c_copied"), sem("c_kv"), sem("x_v_all_ready")
        kh_tr, kh_copied = sem("kh_tr"), sem("kh_copied")
        hn_var, hn_done = sem("hn_var"), sem("hn_done")
        rec_copied = sem("rec_copied")
        front = sem("front")
        x_key_ready, x_v_ready = sem("x_key_ready"), sem("x_v_ready")
        xs_ready, xs_shifted, xs_exp = sem("xs_ready"), sem("xs_shifted"), sem("xs_exp")
        xn_copied = sem("xn_copied")
        g_ready, g_exp, we_ready = sem("g_ready"), sem("g_exp"), sem("we_ready")
        h_ready, h_relu, h_sq, e_ready, e_added = sem("h_ready"), sem("h_relu"), sem("h_sq"), sem("e_ready"), sem("e_added")

        ONE = 1
        PRO = 1 + B
        UNITS = 64

        def blocks():
            return [(n, TB - 1 - n) for n in range(TB)]

        def width(blk, u):
            return (blk * BS + (5 if u in (2, 3) else u + 1)) * 2 * QT

        def units(blk):
            full = [list(range(j, min(j + 2, blk))) for j in range(0, blk, 2)]
            return full + [None]

        def unit_base():
            at, first = 0, {}
            for n, blk in blocks():
                for u in range(BS):
                    first[n, u] = at
                    at += len(units(blk))
            assert at == UNITS
            return first

        first_unit = unit_base()

        def last_unit(s):
            n, u = divmod(s % STEPS, BS)
            return first_unit[n, u] + len(units(TB - 1 - n)) - 1 - (UNITS if s < 0 else 0)

        AFTER = PRO + B * UNITS // 2
        FIRST = (AFTER + 2, AFTER + 1)
        PER = (2 * TB + 2, 2 * TB + 1)

        def group_at(b, t, g):
            last = isinstance(b, int) and b == B - 1
            late = 0 if last else int(t >= 2)
            return FIRST[g % 2] + b * PER[g % 2] + 2 * t + g // 2 + late

        def front_at(b, i):
            if b is None:
                return AFTER + i // 2
            return FIRST[i % 2] + b * PER[i % 2] + (4, 4, 9)[i]

        block = stack.enter_context(nc.Block())

        @block.sync
        def _(sp):
            sp.dma_start(X[:], x.rearrange("b (t p) d -> p (b t) d", p=T)).then_inc(x_loaded, 16)
            sp.dma_start(pa_sb[:], pack_a).then_inc(a_loaded, 16)
            sp.dma_start(rel[0:72, :], rel_base).then_inc(rel_base_loaded, 16)
            sp.dma_start(pb_sb[:], pack_b).then_inc(b_loaded, 16)
            sp.wait_ge(rel0_ready, 1)
            sp.wait_ge(rel_base_loaded, 16)
            for i in range(QT):
                sp.dma_start(rel[HD * i:HD * i + HD, 1 + i:1 + i + P], rel0[:]).then_inc(rel_loaded, 16)
            with sp.Fori(0, B) as b:
                sp.wait_ge(qT_ready, b + 1 + ONE)
                sp.dma_start(q_dram[bass.ds(b, 1), :, T:T + S].rearrange("o p i -> p (o i)"),
                             qT[:, bass.ds(b * S, S)]).then_inc(q_stored, 16)
            sp.wait_ge(q_stored, 16 * B)

            def load_queries(b, first):
                q_now = q_dram[bass.ds(b, 1)]
                for n, blk in blocks():
                    if not (first and n < 2):
                        sp.wait_ge(q_rel_ready, b * TB + n + 1)
                    for i in range(QT):
                        sp.dma_start(q_rep[HD * i:HD * i + HD, n % 2, :, :],
                                     q_now[:, :, (blk + 1) * T:(blk + 2) * T]
                                     .rearrange("o (h d) i -> d (o h) i", d=HD)).then_inc(q_rep_loaded[n % 2], 16)

            load_queries(0, True)
            with sp.Fori(1, B) as b:
                load_queries(b, False)

            sp.wait_ge(y_added, B * TB + ONE)
            sp.dma_start(ctx_sb, ctx_in.rearrange("b m d -> m b d")).then_inc(ctx_loaded, 16)

            with sp.Fori(0, B) as b:
                sp.wait_ge(e_added, (b + 1) * (E + 1) + ONE)
                sp.dma_start(out[bass.ds(b, 1)].rearrange("o (t p) d -> p (o t) d", p=T),
                             X[:, bass.ds(b * TB, TB), :]).then_inc(out_stored, 16)
            sp.wait_ge(out_stored, 16 * B)

        @block.gpsimd
        def _(pool):
            pool.sem_inc(h_sq, ONE)
            nc.gpsimd.memset(V_now[:], 0.0).then_inc(const_ready, 1)
            nc.gpsimd.memset(pt_diag[:], 0.0).then_inc(const_ready, 1)
            pool.wait_ge(b_loaded, 16)
            with pool.Fori(0, B) as b:
                pool.wait_ge(ln_var, b + 1)
                nc.gpsimd.tensor_tensor(X[:, bass.ds(b * TB, TB), :], X[:, bass.ds(b * TB, TB), :],
                                        cb["bo"].unsqueeze(1).to_broadcast([128, TB, D]),
                                        ALU.add).then_inc(bias_added, 1)

            def build_queries(b, first):
                for n, blk in blocks():
                    slot = n % 2
                    if not (first and n < 2):
                        pool.wait_ge(scores_ready, b * STEPS + (n - 1) * BS)
                    nc.gpsimd.tensor_tensor(
                        q_blk[:, slot],
                        qT[:, bass.ds(b * S + blk * T, T)].unsqueeze(2).to_broadcast([128, T, H]),
                        ca["head_mask"].unsqueeze(1).to_broadcast([128, T, H]),
                        ALU.mult).then_inc(q_blk_ready, 1)
                    pool.wait_ge(q_rep_loaded[slot], (b * 2 + n // 2 + 1) * 16 * QT)
                    nc.gpsimd.tensor_tensor(
                        q_rel[0:QT * HD, slot].rearrange("p (g i) h -> p g i h", i=QT),
                        q_rep[:, slot].rearrange("p h (g i) -> p g i h", i=QT),
                        ca["query_mask"][0:QT * HD].unsqueeze(1).unsqueeze(3)
                        .to_broadcast([QT * HD, T // QT, QT, H]),
                        ALU.mult).then_inc(q_rel_ready, 1)
                    if n == 1:
                        pool.wait_ge(psO_ready, PRO + b * TB)
                        for i in range(HQ):
                            ins = nc.gpsimd.tensor_copy(
                                V_now[:].rearrange("p t (q r) c -> p t q r c", r=HQ)[:, :, :, i, i * HD:i * HD + HD],
                                V[:, bass.ds(b * TB, TB)].rearrange("p t (q r) d -> p t q r d", r=HQ)[:, :, :, i, :])
                        ins.then_inc(v_ready, 1)

            pool.wait_ge(const_ready, 2)
            pool.wait_ge(qT_ready, PRO)
            pool.wait_ge(psO_read, PRO)
            build_queries(0, True)
            with pool.Fori(1, B) as b:
                build_queries(b, False)

            def prepare(b):
                pool.wait_ge(ln_var, b + B + 1)
                nc.gpsimd.tensor_tensor(X[:, bass.ds(b * TB, TB), :], X[:, bass.ds(b * TB, TB), :],
                                        cb["xbp"].unsqueeze(1).to_broadcast([128, TB, D]),
                                        ALU.add).then_inc(bias_added, 1)
            def element(b, more):
                if not (isinstance(b, int) and b == 0):
                    pool.wait_ge(xs_ready, b * TB)
                nc.gpsimd.tensor_tensor(x_key, khT[:, bass.ds(b * M, M)].unsqueeze(1).to_broadcast([128, H, M]),
                                        ca["head_mask"].unsqueeze(2).to_broadcast([128, H, M]),
                                        ALU.mult).then_inc(x_key_ready, 1)
                pool.wait_ge(psO_ready, PRO + B * TB + b * TB)
                nc.gpsimd.tensor_copy(x_v, x_v_all[:, bass.ds(b, 1)].rearrange("p o h c -> p (o h) c"))\
                    .then_inc(x_v_ready, 1)
                if more:
                    prepare(b + 1)

            prepare(0)
            pool.wait_ge(kh_copied, 1)
            pool.wait_ge(x_v_all_ready, 1)
            element(0, True)
            with pool.Fori(1, B - 1) as b:
                element(b, True)
            element(B - 1, False)

            def experts(b, more):
                for e in range(E + 1):
                    pool.wait_ge(h_relu, b * (E + 1) + e + 1 + ONE)
                    pool.wait_ge(e_ready, b * (E + 1) + max(e - 1, 0) + ONE)
                    nc.gpsimd.tensor_tensor(hidden[:, e % 2], relu[:, e % 2], relu[:, e % 2],
                                            ALU.mult).then_inc(h_sq, 1)

            with pool.Fori(0, B - 1) as b:
                experts(b, True)
            experts(B - 1, False)

        @block.scalar
        def _(act):
            for started in (*psT_read, scores_read, h_relu):
                act.sem_inc(started, ONE)
            def seed(i, st, groups):
                nc.scalar.activation(st[:, 3, 0:groups], st[:, 2, 0:groups], ACT.Ln).then_inc(seed_log, 1)
                act.wait_ge(seed_log, i + 1)
                nc.scalar.activation(st[:, 5, 0:groups], st[:, 3, 0:groups], ACT.Exp, scale=-0.5).then_inc(seeded, 1)

            act.wait_ge(a_loaded, 16)
            with act.Fori(0, B) as b:
                act.wait_ge(ln_var, b + 1)
                seed(b, stat, TB)
                for half in range(2):
                    act.wait_ge(psT_ready[half], b + 1 + ONE)
                    if half == 0:
                        act.wait_ge(psO_ready, b + ONE)
                    nc.scalar.activation(xnT[:, half * 256:half * 256 + 256], psT[:, half, 0:256],
                                         ACT.Copy).then_inc(psT_read[half], 1)
                act.wait_ge(k_ready, b + 1)
                nc.scalar.activation(kT[:, bass.ds(b * S, S)], psS[:, 1, :], ACT.Identity,
                                     bias=ca["bk"]).then_inc(scores_read, 1)

            with act.Fori(0, B) as b:
                for n, blk in blocks():
                    for u in range(BS):
                        s = n * BS + u
                        wide = width(blk, u)
                        act.wait_ge(max_ready, b * STEPS + s + 1)
                        k = last_unit(s - 4)
                        act.wait_ge(psT_ready[k % 2], PRO + b * (UNITS // 2) + k // 2 + 1)
                        for i in range(2):
                            ins = nc.scalar.activation(prob[:, s % 4, i, 0:wide], psS[:, 2 * (s % 2) + i, 0:wide],
                                                       ACT.Exp, bias=neg_max[:, s % 2, i:i + 1],
                                                       accum_out=row_sum[:, n % 2, 2 * u + i:2 * u + i + 1])
                        ins.then_inc(scores_read, 1)

            def front_copy(b, i, dst):
                n = front_at(b, i)
                act.wait_ge(psT_ready[i % 2], n + 1)
                nc.scalar.activation(dst, psT[:, i % 2, :], ACT.Copy).then_inc(psT_read[i % 2], 1)

            act.wait_ge(c_tr, 1)
            nc.scalar.activation(ctxT, psM[:, 0:B * M], ACT.Copy).then_inc(c_copied, 1)
            act.wait_ge(ln_var, B + 1)
            seed(B, stat, TB)
            front_copy(None, 0, xnT[:])
            act.wait_ge(hn_var, 1)
            seed(B + 1, k_stat, TB * H)
            front_copy(None, 1, x_q2)
            act.wait_ge(kh_tr, 1)
            nc.scalar.activation(khT, psM[:, 0:B * M], ACT.Copy).then_inc(kh_copied, 1)
            act.wait_ge(hn_var, 2)
            seed(B + 2, stat, TB * H)
            front_copy(None, 2, x_qT)

            def x_exp(b, t):
                act.wait_ge(xs_shifted, b * TB + t + 1 + ONE)
                nc.scalar.activation(x_prob[t % 2], x_prob[t % 2], ACT.Exp).then_inc(xs_exp, 1)

            def element(b, more):
                for t in range(TB):
                    for g in range(H // XG):
                        act.wait_ge(psT_ready[g % 2], group_at(b, t, g) + 1)
                        act.wait_ge(psO_ready, PRO + B * TB + b * TB + t)
                        nc.scalar.activation(x_pT[:, g * XG:g * XG + XG, :],
                                             psT[0:M, g % 2, :].rearrange("p (h i) -> p h i", h=XG),
                                             ACT.Copy).then_inc(psT_read[g % 2], 1)
                    if t + 1 < TB:
                        x_exp(b, t + 1)
                    act.wait_ge(sums_ready, B * TB + b * TB + t + 1)
                    nc.scalar.activation(rec[:], psM[:, 0:T], ACT.Copy).then_inc(rec_copied, 1)
                    if more and t == 0:
                        act.wait_ge(ln_var, B + b + 2)
                        seed(b * 2 + B + 3, stat, TB)
                    if more and t == 1:
                        front_copy(b, 0, xnT[:])
                        front_copy(b, 1, x_q2)
                    if more and t == 2:
                        act.wait_ge(hn_var, b + 3)
                        seed(b * 2 + B + 4, stat, TB * H)
                    if more and t == 3:
                        front_copy(b, 2, x_qT)
                        x_exp(b + 1, 0)

            x_exp(0, 0)
            with act.Fori(0, B - 1) as b:
                element(b, True)
            element(B - 1, False)

            def seed_experts(b):
                act.wait_ge(ln_var, 2 * B + b + 1)
                seed(b + 3 * B + 1, stat, TB)

            def front_experts(b):
                act.wait_ge(transposed, b + 1)
                nc.scalar.activation(xnT[:], psO[:], ACT.Copy).then_inc(xn_copied, 1)
                act.wait_ge(g_ready, b + 1)
                nc.scalar.activation(r_exp, psM[:, 0:TB * E], ACT.Exp, scale=-1.0).then_inc(g_exp, 1)

            def experts(b, more):
                for e in range(E + 1):
                    act.wait_ge(h_ready, b * (E + 1) + e + 1)
                    act.wait_ge(h_sq, b * (E + 1) + max(e - 1, 0) + ONE)
                    nc.scalar.activation(relu[:, e % 2], psS[:, e % 4, :], ACT.Relu).then_inc(h_relu, 1)
                    if e == 4 and more:
                        seed_experts(b + 1)
                if more:
                    front_experts(b + 1)

            seed_experts(0)
            front_experts(0)
            with act.Fori(0, B - 1) as b:
                experts(b, True)
            experts(B - 1, False)

        @block.vector
        def _(dve):
            class Chain:

                def __init__(self):
                    self.base, self.n = 0, 0

                def loop(self, i, start, per):
                    self.base, self.n, self.per = start + i * per, 0, per

                def done(self):
                    assert self.n == self.per, self.n

                def link(self, ins):
                    self.n += 1
                    ins.then_inc(vec_step, 1)
                    dve.wait_ge(vec_step, self.base + self.n)

            c = Chain()
            LN, HN = 8, 10
            v = nc.vector

            def refine(st, groups, i):
                var, guess, t = st[:, 2, 0:groups], st[:, 5, 0:groups], st[:, 1, 0:groups]
                dve.wait_ge(seeded, i + 1)
                c.link(v.scalar_tensor_tensor(out=t, in0=var, scalar=-0.5, in1=guess, op0=ALU.mult, op1=ALU.mult))
                c.link(v.tensor_tensor(t, t, guess, ALU.mult))
                c.link(v.scalar_tensor_tensor(out=st[:, 3, 0:groups], in0=t, scalar=1.5, in1=guess,
                                              op0=ALU.add, op1=ALU.mult))

            def layer_norm(b, n, seeds, stage_used=None):
                xt = X[:, bass.ds(b * TB, TB), :]
                c.link(v.reduce_sum(stat[:, 0, 0:TB], xt, AX_X))
                c.link(v.tensor_scalar(stat[:, 4, 0:TB], stat[:, 0, 0:TB], 1.0 / D, None, ALU.mult))
                c.link(v.tensor_tensor(xc[:], xt, stat[:, 4, 0:TB].unsqueeze(2).to_broadcast([128, TB, D]),
                                       ALU.subtract))
                c.link(v.tensor_tensor(sq[:], xc[:], xc[:], ALU.mult))
                c.link(v.reduce_sum(stat[:, 1, 0:TB], sq[:], AX_X))
                v.tensor_scalar(stat[:, 2, 0:TB], stat[:, 1, 0:TB], 1.0 / D, EPS,
                                ALU.mult, ALU.add).then_inc(ln_var, 1)
                refine(stat, TB, seeds)
                if stage_used is not None:
                    dve.wait_ge(psT_ready[1], stage_used)
                v.tensor_tensor(stage[:], xc[:], stat[:, 3, 0:TB].unsqueeze(2).to_broadcast([128, TB, D]),
                                ALU.mult).then_inc(ln_done, 1)

            for started in (qT_ready, psO_read, y_added, xs_shifted, e_added):
                dve.sem_inc(started, ONE)
            dve.wait_ge(a_loaded, 16)
            for slot in range(2):
                rows = slice(QT * HD, QT * HD + QT)
                v.tensor_copy(
                    q_rel[rows, slot].rearrange("p (g i) h -> p g i h", i=QT),
                    ca["query_mask"][rows].unsqueeze(1).unsqueeze(3).to_broadcast([QT, T // QT, QT, H]),
                ).then_inc(q_rel_ready, 1)
            v.tensor_scalar(rel0[:], ca["rel"][0:HD, :], ca["rel"][0:HD, 0:1], None,
                            ALU.subtract).then_inc(rel0_ready, 1)
            dve.wait_ge(x_loaded, 16)

            def project(b):
                dve.wait_ge(q_ready, b + 1)
                v.tensor_scalar(qT[:, bass.ds(b * S, S)], psS[:, 0, :], ca["bq"], SCALE,
                                ALU.add, ALU.mult).then_inc(qT_ready, 1)
                dve.wait_ge(psO_ready, b + 1 + ONE)
                v.tensor_tensor(V[:, bass.ds(b * TB, TB), :, :].rearrange("p t h d -> p t (h d)"),
                                psO[:].rearrange("p (t f) -> p t f", t=TB),
                                ca["bv"].unsqueeze(1).to_broadcast([128, TB, D]), ALU.add).then_inc(psO_read, 1)

            c.loop(0, 0, LN)
            layer_norm(0, 0, 0)
            c.done()
            with dve.Fori(1, B) as b:
                c.loop(b, 0, LN)
                layer_norm(b, b, b, b + ONE)
                project(b - 1)
                c.done()
            project(B - 1)

            def finish(k):
                dve.wait_ge(sums_ready, k + 1)
                c.link(v.reciprocal(rec[:], psM[:, 0:T]))
                dve.wait_ge(psO_ready, PRO + k + 1)
                v.tensor_tensor(oT[:], psO[:, 0:T], rec[:], ALU.mult).then_inc(psO_read, 1)

            def add_y(k, tile):
                dve.wait_ge(y_ready, k + 1)
                xt = X[:, bass.ds(tile, 1), :].rearrange("p o d -> p (o d)")
                v.tensor_tensor(xt, psM[:, T:2 * T], xt, ALU.add).then_inc(y_added, 1)

            dve.wait_ge(bias_added, B)
            dve.wait_ge(const_ready, 2)
            with dve.Fori(0, B) as b:
                c.loop(b, LN * B, TB)

                def copy_units(s):
                    n, u = divmod(s, BS)
                    blk = TB - 1 - n
                    if u == 0:
                        dve.wait_ge(psO_ready, PRO + b * TB + n - 1)
                    for i, js in enumerate(units(blk)):
                        k = first_unit[n, u] + i
                        dve.wait_ge(psT_ready[k % 2], PRO + b * (UNITS // 2) + k // 2 + 1)
                        if js is None:
                            w = width(0, u)
                            dst = pt_diag[0:w, n % 2, :, 2 * QT * u:2 * QT * (u + 1)].rearrange("p h i -> p i h")
                            src = psT[0:w, k % 2, 0:256].rearrange("p (i h) -> p i h", h=H)
                        else:
                            dst = pt_full[n % 2][:, js[0]:js[-1] + 1, :, 2 * QT * u:2 * QT * (u + 1)]\
                                .rearrange("p j h i -> p j i h")
                            src = psT[:, k % 2, 0:256 * len(js)].rearrange("p (j i h) -> p j i h", h=H, i=2 * QT)
                        v.tensor_copy(dst, src).then_inc(psT_read[k % 2], 1)

                def spread_sums(n):
                    dve.wait_ge(scores_read, PRO + b * STEPS + (n + 1) * BS)
                    v.tensor_tensor(spread[:].rearrange("p (t i) -> p t i", i=QT),
                                    row_sum[:, n % 2, :].unsqueeze(2).to_broadcast([128, 2 * BS, QT]),
                                    ca["row_query"].unsqueeze(1).to_broadcast([128, 2 * BS, QT]),
                                    ALU.mult).then_inc(spread_ready, 1)

                for n, blk in blocks():
                    for u in range(BS):
                        s = n * BS + u
                        wide = width(blk, u)
                        if n and u == 2:
                            spread_sums(n - 1)
                        if n and u == BS - 2:
                            finish(b * TB + n - 1)
                        if n > 1 and u == 0:
                            add_y(b * TB + n - 2, b * TB + TB - 1 - (n - 2))
                        dve.wait_ge(scores_ready, b * STEPS + s + 1)
                        v.tensor_reduce(neg_max[:, s % 2], psS[:, 2 * (s % 2):2 * (s % 2) + 2, 0:wide],
                                        AX_X, ALU.max, negate=True).then_inc(max_ready, 1)
                        if s >= 2:
                            copy_units(s - 2)
                add_y(b * TB + TB - 2, b * TB + 1)
                copy_units(STEPS - 2)
                copy_units(STEPS - 1)
                spread_sums(TB - 1)
                finish(b * TB + TB - 1)
                add_y(b * TB + TB - 1, b * TB)
                c.done()

            def head_norm(src, dst, xc_, sq_, st, parts, groups, seeds, b):
                def heads(ap):
                    return ap.rearrange("p (g d) -> p g d", d=HD)

                def spread(row):
                    return st[:, row, 0:groups].unsqueeze(2).to_broadcast([parts, groups, HD])

                if b is None:
                    dve.wait_ge(c_kv, 1)
                elif isinstance(b, int):
                    dve.wait_ge(psT_read[1], front_at(None, 1) + 1)
                else:
                    dve.wait_ge(psT_read[1], front_at(b - 1, 1) + 1)
                c.link(v.reduce_sum(st[:, 0, 0:groups], heads(src), AX_X))
                c.link(v.tensor_scalar(st[:, 4, 0:groups], st[:, 0, 0:groups], 1.0 / HD, None, ALU.mult))
                c.link(v.tensor_tensor(heads(xc_), heads(src), spread(4), ALU.subtract))
                c.link(v.tensor_tensor(sq_, xc_, xc_, ALU.mult))
                c.link(v.reduce_sum(st[:, 1, 0:groups], heads(sq_), AX_X))
                v.tensor_scalar(st[:, 2, 0:groups], st[:, 1, 0:groups], 1.0 / HD, EPS,
                                ALU.mult, ALU.add).then_inc(hn_var, 1)
                refine(st, groups, seeds)
                tiles = groups // H

                def tiled(ap):
                    return ap.rearrange("p (t f) -> p t f", t=tiles)

                c.link(v.tensor_tensor(heads(sq_), heads(xc_), spread(3), ALU.mult))
                c.link(v.tensor_tensor(tiled(xc_), tiled(sq_),
                                       cb["ln_g"][0:parts].unsqueeze(1).to_broadcast([parts, tiles, D]), ALU.mult))
                v.tensor_tensor(tiled(dst), tiled(xc_),
                                cb["ln_b"][0:parts].unsqueeze(1).to_broadcast([parts, tiles, D]),
                                ALU.add).then_inc(hn_done, 1)

            def prepare(b, k):
                layer_norm(b, b + B, B)
                if k == 0:
                    head_norm(psS[0:M, 0, :], x_k, k_c, k_sq, k_stat, M, TB * H, B + 1, None)
                head_norm(x_q2, x_q, xc[:].rearrange("p t d -> p (t d)"), sq[:].rearrange("p t d -> p (t d)"),
                          stat, 128, TB * H, B + 2, b)

            START = LN * B + TB * B
            c.loop(0, START, 1 + LN + 2 * HN)
            c.link(v.memset(pt_diag[0:M, 0, :, :], 0.0))
            prepare(0, 0)
            dve.wait_ge(c_kv, 1)
            for i in range(HQ):
                ins = v.tensor_copy(x_v_all.rearrange("p b (q r) c -> p b q r c", r=HQ)[:, :, :, i, i * HD:i * HD + HD],
                                    psS[0:M, 1, :].rearrange("p (b q r d) -> p b q r d", b=B, r=HQ, d=HD)[:, :, :, i, :])
            ins.then_inc(x_v_all_ready, 1)
            c.done()
            START += 1 + LN + 2 * HN

            def shift(b, t):
                dve.wait_ge(xs_ready, b * TB + t + 1)
                sc = psS[:, :, 0:XG * M].rearrange("p g (h j) -> p g h j", h=XG)
                c.link(v.tensor_reduce(x_max, sc, AX_X, ALU.max, negate=True))
                v.tensor_tensor(x_prob[t % 2].rearrange("p (g h) j -> p g h j", h=XG), sc,
                                x_max.rearrange("p (g h) -> p g h", h=XG).unsqueeze(3)
                                .to_broadcast([128, H // XG, XG, M]), ALU.add).then_inc(xs_shifted, 1)

            def element(b, more):
                for t in range(TB):
                    k = B * TB + b * TB + t
                    if t + 1 < TB:
                        shift(b, t + 1)
                    dve.wait_ge(xs_exp, b * TB + t + 1)
                    c.link(v.reduce_sum(x_sum, x_prob[t % 2], AX_X))
                    c.link(v.reciprocal(x_sum, x_sum))
                    v.tensor_copy(spread[:].rearrange("p (h d) -> p h d", h=H),
                                  x_sum.unsqueeze(2).to_broadcast([128, H, HD])).then_inc(spread_ready, 1)
                    if t:
                        add_y(k - 1, b * TB + t - 1)
                    dve.wait_ge(rec_copied, b * TB + t + 1)
                    dve.wait_ge(psO_ready, PRO + k + 1)
                    v.tensor_tensor(oT[:], psO[:, 0:T], rec[:], ALU.mult).then_inc(psO_read, 1)
                    if t == 0 and more:
                        layer_norm(b + 1, b + 1 + B, b * 2 + B + 3)
                        dve.wait_ge(bias_added, B + b + 2)
                    if t == 2 and more:
                        head_norm(x_q2, x_q, xc[:].rearrange("p t d -> p (t d)"),
                                  sq[:].rearrange("p t d -> p (t d)"), stat, 128, TB * H, b * 2 + B + 4, b + 1)
                if more:
                    shift(b + 1, 0)
                add_y(B * TB + b * TB + TB - 1, b * TB + TB - 1)

            c.loop(0, START, 1)
            shift(0, 0)
            c.done()
            START += 1
            dve.wait_ge(bias_added, B + 1)
            with dve.Fori(0, B - 1) as b:
                c.loop(b, START, 3 * TB + LN + HN)
                element(b, True)
                c.done()
            START += (B - 1) * (3 * TB + LN + HN)
            c.loop(0, START, 3 * TB - 1)
            element(B - 1, False)
            c.done()
            START += 3 * TB - 1

            def route(b):
                dve.wait_ge(g_exp, b + 1)
                c.link(v.tensor_tensor(r_z.rearrange("p (t e) -> p t e", t=TB),
                                       psM[:, 0:TB * E].rearrange("p (t e) -> p t e", t=TB),
                                       cb["lb"].unsqueeze(1).to_broadcast([128, TB, E]), ALU.add))
                mine = r_z.unsqueeze(2).to_broadcast([128, TB * E, E])
                other = r_z.rearrange("p (t e) -> p t e", t=TB).unsqueeze(2).to_broadcast([128, TB, E, E])
                mine4 = mine.rearrange("p (t e) f -> p t e f", t=TB)
                c.link(v.tensor_tensor(r_gt.rearrange("p (t e f) -> p t e f", t=TB, e=E), mine4, other, ALU.is_lt))
                c.link(v.tensor_tensor(r_eq.rearrange("p (t e f) -> p t e f", t=TB, e=E), mine4, other, ALU.is_equal))
                before = cb["before"].unsqueeze(1).to_broadcast([128, TB, E * E])
                eq = r_eq.rearrange("p (t f) -> p t f", t=TB)
                c.link(v.tensor_tensor(eq, eq, before, ALU.mult))
                c.link(v.tensor_tensor(r_gt, r_gt, r_eq, ALU.add))
                c.link(v.reduce_sum(r_rank, r_gt.rearrange("p (g f) -> p g f", f=E), AX_X))
                c.link(v.tensor_scalar(r_sig, r_exp, 1.0, None, ALU.add))
                c.link(v.reciprocal(r_sig, r_sig))
                c.link(v.scalar_tensor_tensor(out=r_w, in0=r_rank, scalar=2.0, in1=r_sig,
                                              op0=ALU.is_lt, op1=ALU.mult))
                w3 = r_w.rearrange("p (t e) -> p t e", t=TB)
                c.link(v.reduce_sum(r_sum, w3, AX_X))
                c.link(v.tensor_scalar(r_sum, r_sum, 1e-6, None, ALU.add))
                v.reciprocal(r_inv, r_sum).then_inc(we_ready, 1)
                dve.wait_ge(we_ready, 2 * b + 1)
                v.tensor_tensor(r_we.rearrange("p (t e) -> p t e", t=TB), w3,
                                r_inv.unsqueeze(2).to_broadcast([128, TB, E]), ALU.mult).then_inc(we_ready, 1)

            def experts(b, more):
                dve.wait_ge(we_ready, 2 * b + 2)
                for e in range(E + 1):
                    dve.wait_ge(e_ready, b * (E + 1) + e + 1 + ONE)
                    dve.wait_ge(e_added, b * (E + 1) + e + ONE)
                    if e == E:
                        xt = X[:, bass.ds(b * TB, TB), :]
                        v.tensor_tensor(xt, psT[:, e % 2, :].rearrange("p (t d) -> p t d", t=TB), xt,
                                        ALU.add).then_inc(e_added, 1)
                        continue
                    for t in range(TB):
                        xt = X[:, bass.ds(b * TB + t, 1), :].rearrange("p o d -> p (o d)")
                        ins = v.scalar_tensor_tensor(out=xt, in0=psT[:, e % 2, t * T:t * T + T],
                                                     scalar=r_we[:, t * E + e:t * E + e + 1], in1=xt,
                                                     op0=ALU.mult, op1=ALU.add)
                    ins.then_inc(e_added, 1)
                    if e == 2 and more:
                        layer_norm(b + 1, b + 1 + 2 * B, b + 3 * B + 2)
                if more:
                    route(b + 1)

            c.loop(0, START, LN + 11)
            layer_norm(0, 2 * B, 3 * B + 1)
            route(0)
            c.done()
            with dve.Fori(0, B - 1) as b:
                c.loop(b, START + LN + 11, LN + 11)
                experts(b, True)
                c.done()
            experts(B - 1, False)

        @block.tensor
        def _(pe):
            mm = nc.tensor.matmul

            for started in (*psT_ready, psO_ready, e_ready):
                pe.sem_inc(started, ONE)
            pe.wait_ge(a_loaded, 16)
            with pe.Fori(0, B) as b:
                pe.wait_ge(ln_done, b + 1)
                for half in range(2):
                    pe.wait_ge(psT_read[half], b + ONE)
                    for i in range(2):
                        ins = nc.tensor.transpose(psT[:, half, i * T:i * T + T], stage[:, 2 * half + i, :], ident)
                    ins.then_inc(psT_ready[half], 1)
                for half in range(2):
                    pe.wait_ge(psT_read[half], b + 1 + ONE)
                pe.wait_ge(qT_ready, b + ONE)
                mm(psS[:, 0, :], ca["wq"], xnT[:], start=True, stop=True).then_inc(q_ready, 1)
                pe.wait_ge(scores_read, b + ONE)
                mm(psS[:, 1, :], ca["wk"], xnT[:], start=True, stop=True).then_inc(k_ready, 1)
                pe.wait_ge(psO_read, b + ONE)
                for t in range(TB):
                    ins = mm(psO[:, t * D:t * D + D], xnT[:, t * T:t * T + T], ca["wv"], start=True, stop=True)
                ins.then_inc(psO_ready, 1)

            def attend(quadrant, parts, last):
                n = 0
                for i in range(HQ):
                    mine = parts(quadrant * HQ + i)
                    for val, w in mine:
                        ins = mm(psO[quadrant * 32:quadrant * 32 + 32, 0:T], val, w,
                                 start=(n == 0), stop=(n == HQ * len(mine) - 1))
                        n += 1
                if last:
                    ins.then_inc(psO_ready, 1)

            def project_o(k, w):
                pe.wait_ge(psO_read, PRO + k + 1)
                mm(psM[:, T:2 * T], oT[:], w, start=True, stop=True).then_inc(y_ready, 1)

            pe.wait_ge(rel_loaded, 16 * QT)
            pe.wait_ge(b_loaded, 16)
            pe.wait_ge(qT_ready, PRO)
            pe.wait_ge(psO_read, PRO)
            pe.wait_ge(scores_read, PRO)
            with pe.Fori(0, B) as b:
                def scores(s):
                    n, u = divmod(s, BS)
                    blk = TB - 1 - n
                    wide = width(blk, u)
                    if u == 0:
                        pe.wait_ge(q_blk_ready, b * TB + n + 1)
                        pe.wait_ge(q_rel_ready, b * TB + n + 3)
                    pe.wait_ge(scores_read, PRO + b * STEPS + s - 1)
                    for r in range(2):
                        q0 = (2 * u + r) * QT
                        i0 = blk * T + q0
                        lo = max(0, i0 - P)
                        dst = psS[:, 2 * (s % 2) + r, :]
                        mm(dst[:, 0:wide], q_blk[:, n % 2, q0:q0 + QT, :].rearrange("p i h -> p (i h)"),
                           kT[:, bass.ds(b * S, wide)], start=True, stop=False)
                        ins = mm(dst[:, lo:wide],
                                 q_rel[0:QT * HD + QT, n % 2, q0:q0 + QT, :].rearrange("p i h -> p (i h)"),
                                 rel[0:QT * HD + QT, lo - i0 + P:wide - i0 + P], start=False, stop=True)
                    ins.then_inc(scores_ready, 1)

                def transpose_weights(s):
                    n, u = divmod(s, BS)
                    blk = TB - 1 - n
                    pe.wait_ge(scores_read, PRO + b * STEPS + s + 1)
                    for i, js in enumerate(units(blk)):
                        k = first_unit[n, u] + i
                        pe.wait_ge(psT_read[k % 2], PRO + b * (UNITS // 2) + k // 2)
                        w = T if js else width(0, u)
                        for jn, j in enumerate(js or [blk]):
                            for r in range(2):
                                at = (jn * 2 + r) * T
                                ins = nc.tensor.transpose(psT[0:w, k % 2, at:at + T],
                                                          prob[:, s % 4, r, j * T:j * T + w], ident)
                        ins.then_inc(psT_ready[k % 2], 1)

                def copied(n):
                    last = first_unit[n, BS - 1] + len(units(TB - 1 - n)) - 1
                    for k in (last - 1, last):
                        pe.wait_ge(psT_read[k % 2], PRO + b * (UNITS // 2) + k // 2 + 1)

                def attend_block(n, quadrant):
                    blk = TB - 1 - n
                    k = b * TB + n
                    if quadrant == 0:
                        if n == 0:
                            pe.wait_ge(v_ready, b + 1)
                        copied(n)
                        pe.wait_ge(psO_read, PRO + k)

                    def parts(h):
                        return [(V_now[:, j, h, :], pt_full[n % 2][:, j, h, :]) for j in range(blk)] + \
                               [(V_now[:, blk, h, :], pt_diag[:, n % 2, h, :])]

                    attend(quadrant, parts, quadrant == 3)

                def sum_rows(k):
                    pe.wait_ge(spread_ready, k + 1)
                    pe.wait_ge(y_added, k + ONE)
                    mm(psM[:, 0:T], ca["row_head"], spread[:], start=True, stop=True).then_inc(sums_ready, 1)

                for s in range(STEPS):
                    n, u = divmod(s, BS)
                    scores(s)
                    if s >= 2:
                        transpose_weights(s - 2)
                    if n and 2 <= u <= 5:
                        attend_block(n - 1, u - 2)
                    if n and u == 4:
                        sum_rows(b * TB + n - 1)
                    if n and u == 7:
                        project_o(b * TB + n - 1, cb["wo"])
                transpose_weights(STEPS - 2)
                transpose_weights(STEPS - 1)
                sum_rows(b * TB + TB - 1)
                for quadrant in range(4):
                    attend_block(TB - 1, quadrant)
                project_o(b * TB + TB - 1, cb["wo"])

            pe.wait_ge(y_added, B * TB + ONE)
            pe.wait_ge(ctx_loaded, 16)
            for b in range(B):
                ins = nc.tensor.transpose(psM[:, b * M:b * M + M], ctx_sb[:, b, :], ident[0:M, 0:M])
            ins.then_inc(c_tr, 1)

            def front_tokens(b, k):
                pe.wait_ge(ln_done, B + k + 1)
                pe.wait_ge(psT_read[0], front_at(b, 0))
                for t in range(TB):
                    ins = nc.tensor.transpose(psT[:, 0, t * T:t * T + T], stage[:, t, :], ident)
                ins.then_inc(psT_ready[0], 1)

            def front_queries(b):
                pe.wait_ge(psT_read[0], front_at(b, 0) + 1)
                pe.wait_ge(psT_read[1], front_at(b, 1))
                for t in range(TB):
                    ins = mm(psT[:, 1, t * D:t * D + D], xnT[:, t * T:t * T + T], cb["xwq"], start=True, stop=True)
                ins.then_inc(psT_ready[1], 1)

            def front_transpose(b, k):
                pe.wait_ge(hn_done, k + 2)
                pe.wait_ge(psT_read[0], front_at(b, 2))
                for t in range(TB):
                    ins = nc.tensor.transpose(psT[:, 0, t * T:t * T + T], x_q[:, t * T:t * T + T], ident)
                ins.then_inc(psT_ready[0], 1)

            pe.wait_ge(c_copied, 1)
            for b in range(B):
                mm(psS[0:M, 0, b * D:b * D + D], ctxT[:, b * M:b * M + M], cb["xwk"], start=True, stop=True)
            for b in range(B):
                ins = mm(psS[0:M, 1, b * D:b * D + D], ctxT[:, b * M:b * M + M], cb["xwv"], start=True, stop=True)
            ins.then_inc(c_kv, 1)
            front_tokens(None, 0)
            front_queries(None)
            pe.wait_ge(hn_done, 1)
            for b in range(B):
                ins = nc.tensor.transpose(psM[:, b * M:b * M + M], x_k[:, b * D:b * D + D], ident[0:M, 0:M])
            ins.then_inc(kh_tr, 1)
            front_transpose(None, 0)
            pe.wait_ge(x_v_all_ready, 1)
            pe.wait_ge(kh_copied, 1)

            def x_scores(b, t):
                if t == 0:
                    pe.wait_ge(x_key_ready, b + 1)
                    pe.wait_ge(psT_read[0], AFTER + 2 if isinstance(b, int) else FIRST[0] + b * PER[0])
                pe.wait_ge(xs_shifted, b * TB + t + ONE)
                for g in range(H // XG):
                    ins = mm(psS[:, g, 0:XG * M], x_qT[:, t * T:t * T + T],
                             x_key[:, g * XG:g * XG + XG, :].rearrange("p h j -> p (h j)"),
                             start=True, stop=True)
                ins.then_inc(xs_ready, 1)

            def element(b, more):
                for t in range(TB):
                    k = B * TB + b * TB + t
                    if t + 1 < TB:
                        x_scores(b, t + 1)
                    pe.wait_ge(xs_exp, b * TB + t + 1)
                    for g in range(H // XG):
                        pe.wait_ge(psT_read[g % 2], group_at(b, t, g))
                        for i in range(XG):
                            ins = nc.tensor.transpose(psT[0:M, g % 2, i * T:i * T + T],
                                                      x_prob[t % 2][:, g * XG + i, :], ident)
                        ins.then_inc(psT_ready[g % 2], 1)
                    if t:
                        project_o(k - 1, cb["xwp"])
                    if t == 1 and more:
                        front_tokens(b, b + 1)
                    if t == 3 and more:
                        front_transpose(b, b + 1)
                    if t == 0:
                        pe.wait_ge(x_v_ready, b + 1)
                    for g in (2, 3):
                        pe.wait_ge(psT_read[g % 2], group_at(b, t, g) + 1)
                    pe.wait_ge(psO_read, PRO + k)
                    for quadrant in range(4):
                        attend(quadrant, lambda h: [(x_v[:, h, :], x_pT[:, h, :])], quadrant == 3)
                    pe.wait_ge(spread_ready, k + 1)
                    pe.wait_ge(y_added, k + ONE)
                    nc.tensor.transpose(psM[:, 0:T], spread[:], ident).then_inc(sums_ready, 1)
                    if t == 1 and more:
                        front_queries(b)
                if more:
                    x_scores(b + 1, 0)
                project_o(B * TB + b * TB + TB - 1, cb["xwp"])

            x_scores(0, 0)
            with pe.Fori(0, B - 1) as b:
                element(b, True)
            element(B - 1, False)

            pe.wait_ge(y_added, 2 * B * TB + ONE)

            def front_experts(b):
                pe.wait_ge(ln_done, 2 * B + b + 1)
                for t in range(TB):
                    ins = nc.tensor.transpose(psO[:, t * T:t * T + T], stage[:, t, :], ident)
                ins.then_inc(transposed, 1)

            def gate(b):
                pe.wait_ge(xn_copied, b + 1)
                for t in range(TB):
                    ins = mm(psM[:, t * E:t * E + E], xnT[:, t * T:t * T + T], cb["gate"], start=True, stop=True)
                ins.then_inc(g_ready, 1)

            def experts(b, more):
                def up(e):
                    pe.wait_ge(h_relu, b * (E + 1) + max(e - 3, 0) + ONE)
                    mm(psS[:, e % 4, :], cb["w1"][:, e * D:e * D + D], xnT[:], start=True, stop=True)\
                        .then_inc(h_ready, 1)

                up(0)
                up(1)
                for e in range(E + 1):
                    if e + 2 < E + 1:
                        up(e + 2)
                    if e == E - 1 and more:
                        front_experts(b + 1)
                    pe.wait_ge(h_sq, b * (E + 1) + e + 1 + ONE)
                    pe.wait_ge(e_added, b * (E + 1) + max(e - 1, 0) + ONE)
                    for t in range(TB):
                        ins = mm(psT[:, e % 2, t * D:t * D + D], hidden[:, e % 2, t * T:t * T + T],
                                 cb["w2"][:, e * D:e * D + D], start=True, stop=True)
                    ins.then_inc(e_ready, 1)
                if more:
                    pe.wait_ge(we_ready, 2 * b + 2)
                    gate(b + 1)

            front_experts(0)
            gate(0)
            with pe.Fori(0, B - 1) as b:
                experts(b, True)
            experts(B - 1, False)


def pack(parts, spec):
    width = sum(w for _, w in spec)
    out, at = np.zeros((128, width), np.float32), 0
    for name, w in spec:
        a = parts[name]
        out[0:a.shape[0], at:at + w] = a
        at += w
    return out


def kernel(**inputs):
    import concourse.bacc as bacc
    from concourse.bass_utils import run_bass_kernel_spmd

    a = {n: np.asarray(v) for n, v in inputs.items()}

    def rows(v):
        return np.broadcast_to(v.reshape(1, -1), (128, v.size))

    part = np.arange(128)
    head_mask = (part[:, None] // HD == np.arange(H)[None, :]).astype(np.float32)
    query_mask = np.zeros((128, QT), np.float32)
    query_mask[:QT * HD] = part[:QT * HD, None] // HD == np.arange(QT)[None, :]
    query_mask[QT * HD:QT * HD + QT] = np.eye(QT)
    before = np.broadcast_to((np.arange(E)[None, :] < np.arange(E)[:, None]).astype(np.float32).reshape(1, -1),
                             (128, E * E))
    row_query = (part[:, None] // H == np.arange(QT)[None, :]).astype(np.float32)
    row_head = (part[:, None] % H == part[None, :] // HD).astype(np.float32)
    rel_base = np.zeros((72, RW), np.float32)
    ahead = np.arange(RW)[None, :] - P - np.arange(QT)[:, None] > 0
    rel_base[QT * HD:] = np.where(ahead, np.float32(MASKED), np.float32(0.0))

    pack_a = pack({
        "ident": np.eye(128, dtype=np.float32), "wq": a["L0_attn_Wq"], "wk": a["L0_attn_Wk"],
        "wv": a["L0_attn_Wv"], "bv": rows(a["L0_attn_bv"]), "bq": a["L0_attn_bq"].reshape(D, 1),
        "bk": a["L0_attn_bk"].reshape(D, 1), "head_mask": head_mask, "query_mask": query_mask,
        "rel": a["L0_attn_rel_key"].T, "row_query": row_query, "row_head": row_head}, PACK_A)
    pack_b = pack({
        "wo": a["L0_attn_Wo"], "bo": rows(a["L0_attn_bo"]), "xwq": a["L0_xattn_Wq"].T,
        "xwk": a["L0_xattn_Wk"].T, "xwv": a["L0_xattn_Wv"].T, "xwp": a["L0_xattn_Wp"].T,
        "xbp": rows(a["L0_xattn_bp"]), "ln_g": rows(np.tile(a["L0_xattn_ln_g"], H)),
        "ln_b": rows(np.tile(a["L0_xattn_ln_b"], H)), "gate": a["L0_ffn_gate_w"].T,
        "lb": rows(a["L0_ffn_lb_bias"]), "before": before,
        "w1": np.concatenate([w.T for w in a["L0_ffn_w1"]] + [a["L0_ffn_cfc"].T], axis=1),
        "w2": np.concatenate([w.T for w in a["L0_ffn_w2"]] + [a["L0_ffn_cproj"].T], axis=1)}, PACK_B)

    nc = bacc.Bacc("TRN2", target_bir_lowering=False, num_devices=1)
    arrays = {"x": a["x"], "ctx": a["ctx_1024"], "pack_a": pack_a, "pack_b": pack_b, "rel_base": rel_base}
    arrays = {n: np.ascontiguousarray(v) for n, v in arrays.items()}
    aps = [nc.dram_tensor(n + "_dram", v.shape, mybir.dt.from_np(v.dtype), kind="ExternalInput").ap()
           for n, v in arrays.items()]
    out = nc.dram_tensor("out_dram", (B, S, D), F32, kind="ExternalOutput").ap()
    build(nc, *aps, out)
    r = run_bass_kernel_spmd(nc, [{n + "_dram": v for n, v in arrays.items()}], core_ids=[0])
    return r.results[0]["out_dram"]
```

```python
from contextlib import ExitStack

import numpy as np

import concourse.bass as bass
from concourse import mybir

F32 = mybir.dt.float32
ALU = mybir.AluOpType
ACT = mybir.ActivationFunctionType
AX_X = mybir.AxisListType.X

B, S, D = 4, 512, 128
H, HD = 16, 8
HQ = 4
M = 77
E = 8
P = 256
T = 128
TB = S // T
QT = T // H
STEPS = S // (2 * QT)
BS = T // (2 * QT)
SCALE = HD ** -0.5
EPS = 1e-5
RW = P + 6 * QT
MASKED = -(2.0 ** 100)
XG = 4
XW = H * M
XC = -(-XW // T)
TAIL = XW - (XC - 1) * T
GROUPS = [list(range(g, min(g + 4, XC))) for g in range(0, XC, 4)]

PACK_A = [("ident", T), ("wq", D), ("wk", D), ("wv", D), ("bv", D), ("bq", 1), ("bk", 1),
          ("head_mask", H), ("query_mask", QT), ("rel", P), ("row_query", QT), ("row_head", D)]
PACK_B = [("wo", D), ("bo", D), ("xwq", D), ("xwk", D), ("xwv", D), ("xwp", D), ("xbp", D),
          ("ln_g", 1), ("ln_b", 1), ("chunk_head", XC * H), ("gate", E), ("lb", E), ("before", E * E),
          ("w1", (E + 1) * D), ("w2", (E + 1) * D)]


def columns(pack):
    at, out = 0, {}
    for name, width in pack:
        out[name] = (at, at + width)
        at += width
    return out, at


def build(nc, x, ctx_in, pack_a, pack_b, rel_base, out):
    cols_a, wide_a = columns(PACK_A)
    cols_b, wide_b = columns(PACK_B)
    q_dram = nc.dram_tensor("q_scratch", (B, D, T + S), F32, kind="Internal").ap()
    v_dram = nc.dram_tensor("v_scratch", (B, H, M, HD), F32, kind="Internal").ap()

    with ExitStack() as stack:
        def sb(name, shape):
            return stack.enter_context(nc.sbuf_tensor(name, shape, F32))

        def sem(name):
            return stack.enter_context(nc.semaphore(name))

        pa_sb = sb("pack_a_sb", [128, wide_a])
        pb_sb = sb("pack_b_sb", [128, wide_b])
        ca = {n: pa_sb[:, a:z] for n, (a, z) in cols_a.items()}
        cb = {n: pb_sb[:, a:z] for n, (a, z) in cols_b.items()}
        ident = ca["ident"]

        X = sb("X", [128, B * TB, D])
        stage = sb("stage", [128, TB, D])
        xc = sb("xc", [128, TB, D])
        sq = sb("sq", [128, TB, D])
        xnT = sb("xnT", [128, S])
        stat = sb("stat", [128, 6, TB * H])
        qT = sb("qT", [128, B * S])
        kT = sb("kT", [128, B * S])
        V = sb("V", [128, B * TB, H, HD])
        V_now = sb("V_now", [128, TB, H, HQ * HD])
        rel0 = sb("rel0", [HD, P])
        rel = sb("rel_shifted", [128, RW])
        q_rep = sb("q_rep", [QT * HD, 2, H, T])
        q_blk = sb("q_blk", [128, 2, T, H])
        q_rel = sb("q_rel", [128, 2, T, H])
        prob = sb("prob", [128, 4, 2, S])
        pt_even = sb("pt_even", [128, 3, H, T])
        pt_odd = sb("pt_odd", [128, 1, H, T])
        pt_diag = sb("pt_diag", [128, 2, H, T])
        pt_full = [pt_even, pt_odd]
        ctx_k = sb("ctx_k", [M, B * D])
        ctx_v = sb("ctx_v", [M, B * D])
        v_rows = sb("v_rows", [128, B, XC, HD])
        neg_max = sb("neg_max", [128, 2, 2])
        row_sum = sb("row_sum", [128, 2, 2 * BS])
        spread = sb("spread", [128, T])
        oT = sb("oT", [128, T])
        rec = sb("rec", [128, T])

        prob_flat = prob[:].rearrange("p a b c -> p (a b c)")
        x_flat = [prob_flat[:, i * XW:(i + 1) * XW] for i in range(2)]
        x_prob = [prob_flat[:, i * H * M:(i + 1) * H * M].rearrange("p (h j) -> p h j", h=H)
                  for i in range(2)]
        diag_flat = pt_diag[:].rearrange("p a h i -> p (a h i)")
        x_pT = [a.rearrange("p (c i) -> p c i", c=XC) for a in
                (pt_odd[:].rearrange("p a h i -> p (a h i)")[:, 0:XC * T], diag_flat[:, XC * T:2 * XC * T])]
        x_v = diag_flat[:, 0:XC * T].rearrange("p (c f) -> p c f", c=XC)
        x_key = q_blk[:].rearrange("p a b c -> p (a b c)")[:, 0:H * M].rearrange("p (h j) -> p h j", h=H)
        scratch = pt_even[:].rearrange("p a b c -> p (a b c)")
        names, at = {}, 0
        for name, rows, width in (("x_q", 128, 512), ("x_qT", 128, 512), ("x_q2", 128, 512), ("ctx", M, 512),
                                  ("ctxT", 128, B * M), ("k_c", M, 512), ("k_sq", M, 512),
                                  ("khT", 128, B * M), ("k_stat", M, 384), ("x_max", 128, H), ("x_sum", 128, H)):
            names[name] = scratch[0:rows, at:at + width]
            at += width
        x_q, x_qT, x_q2, ctxT, k_c, k_sq, khT, x_max, x_sum = (
            names[n] for n in ("x_q", "x_qT", "x_q2", "ctxT", "k_c", "k_sq", "khT", "x_max", "x_sum"))
        ctx_sb = names["ctx"].rearrange("p (b d) -> p b d", b=B)
        k_stat = names["k_stat"].rearrange("p (a b) -> p a b", a=6)
        xnT_next = qT[:, 0:S]
        relu = prob_flat[:, 0:1024].rearrange("p (a b) -> p a b", a=2)
        hidden = prob_flat[:, 1024:2048].rearrange("p (a b) -> p a b", a=2)
        rt = scratch[:, 5120:6144]
        r_exp, r_z, r_rank, r_sel = (rt[:, 32 * i:32 * i + 32] for i in range(4))
        r_sig, r_w, r_we = (rt[:, 32 * i:32 * i + 32] for i in range(4, 7))
        r_sum, r_inv = rt[:, 240:244], rt[:, 244:248]
        r_gt, r_eq = rt[:, 256:512], rt[:, 512:768]

        psS = stack.enter_context(nc.psum_tensor("psS", [128, 4, 512], F32))
        psT = stack.enter_context(nc.psum_tensor("psT", [128, 2, 512], F32))
        psO = stack.enter_context(nc.psum_tensor("psO", [128, 512], F32))
        psM = stack.enter_context(nc.psum_tensor("psM", [128, 512], F32))

        a_loaded, b_loaded, x_loaded = sem("a_loaded"), sem("b_loaded"), sem("x_loaded")
        rel_base_loaded, rel_loaded = sem("rel_base_loaded"), sem("rel_loaded")
        q_stored, out_stored = sem("q_stored"), sem("out_stored")
        q_rep_loaded = [sem("q_rep_loaded0"), sem("q_rep_loaded1")]
        ctx_loaded = sem("ctx_loaded")
        const_ready = sem("const_ready")
        rel0_ready = sem("rel0_ready")
        vec_step = sem("vec_step")
        ln_var = sem("ln_var")
        seed_log = sem("seed_log")
        seeded = sem("seeded")
        ln_done = sem("ln_done")
        bias_added = sem("bias_added")
        transposed = sem("transposed")
        psT_read = [sem("psT_read0"), sem("psT_read1")]
        psT_ready = [sem("psT_ready0"), sem("psT_ready1")]
        q_ready, k_ready = sem("q_ready"), sem("k_ready")
        qT_ready = sem("qT_ready")
        v_ready = sem("v_ready")
        q_blk_ready, q_rel_ready = sem("q_blk_ready"), sem("q_rel_ready")
        scores_ready, max_ready = sem("scores_ready"), sem("max_ready")
        scores_read = sem("scores_read")
        psO_ready, psO_read = sem("psO_ready"), sem("psO_read")
        spread_ready, sums_ready = sem("spread_ready"), sem("sums_ready")
        y_ready, y_added = sem("y_ready"), sem("y_added")
        c_tr, c_copied, c_kv = sem("c_tr"), sem("c_copied"), sem("c_kv")
        ctx_v_stored, v_rows_loaded = sem("ctx_v_stored"), sem("v_rows_loaded")
        kh_tr, kh_copied = sem("kh_tr"), sem("kh_copied")
        hn_var, hn_done = sem("hn_var"), sem("hn_done")
        ctx_v_copied = sem("ctx_v_copied")
        rec_copied = sem("rec_copied")
        x_key_ready, x_v_ready = sem("x_key_ready"), sem("x_v_ready")
        xs_ready, xs_shifted, xs_exp = sem("xs_ready"), sem("xs_shifted"), sem("xs_exp")
        xn_copied, xn_moved = sem("xn_copied"), sem("xn_moved")
        g_ready, g_exp, we_ready = sem("g_ready"), sem("g_exp"), sem("we_ready")
        h_ready, h_relu, h_sq, e_ready, e_added = sem("h_ready"), sem("h_relu"), sem("h_sq"), sem("e_ready"), sem("e_added")

        ONE = 1
        PRO = 1 + B
        UNITS = 64

        ORDER = [TB - 2, 1, TB - 1, 0]

        def blocks():
            return list(enumerate(ORDER))

        def width(blk, u):
            return (blk * BS + (5 if u in (2, 3) else u + 1)) * 2 * QT

        def units(blk):
            full = [list(range(j, min(j + 2, blk))) for j in range(0, blk, 2)]
            return full + [None]

        def unit_base():
            at, first = 0, {}
            for n, blk in blocks():
                for u in range(BS):
                    first[n, u] = at
                    at += len(units(blk))
            assert at == UNITS
            return first

        first_unit = unit_base()

        def last_unit(s):
            n, u = divmod(s % STEPS, BS)
            return first_unit[n, u] + len(units(ORDER[n])) - 1 - (UNITS if s < 0 else 0)

        NG = len(GROUPS)
        assert NG * TB % 2 == 0
        AFTER = PRO + B * UNITS // 2
        FIRST = (AFTER + 2, AFTER + 1)
        PER = (NG * TB // 2 + 2, NG * TB // 2 + 1)

        def bank(t, g):
            return (NG * t + g) % 2

        def group_at(b, t, g):
            last = isinstance(b, int) and b == B - 1
            late = 0 if last else (int(t >= 1) + int(t >= 3), int(t >= 2))[bank(t, g)]
            return FIRST[bank(t, g)] + b * PER[bank(t, g)] + (NG * t + g) // 2 + late

        def front_at(b, i):
            if b is None:
                return AFTER + i // 2
            return FIRST[i % 2] + b * PER[i % 2] + (-(-NG // 2), NG, -(-3 * NG // 2) + 1)[i]

        block = stack.enter_context(nc.Block())

        @block.sync
        def _(sp):
            sp.dma_start(X[:], x.rearrange("b (t p) d -> p (b t) d", p=T)).then_inc(x_loaded, 16)
            sp.dma_start(pa_sb[:], pack_a).then_inc(a_loaded, 16)
            sp.dma_start(rel[0:72, :], rel_base).then_inc(rel_base_loaded, 16)
            sp.dma_start(ctx_sb, ctx_in.rearrange("b m d -> m b d")).then_inc(ctx_loaded, 16)
            sp.dma_start(pb_sb[:], pack_b).then_inc(b_loaded, 16)
            sp.wait_ge(rel0_ready, 1)
            sp.wait_ge(rel_base_loaded, 16)
            for i in range(QT):
                sp.dma_start(rel[HD * i:HD * i + HD, 1 + i:1 + i + P], rel0[:]).then_inc(rel_loaded, 16)

            def store_queries(b):
                sp.wait_ge(qT_ready, b + 1 + ONE)
                sp.dma_start(q_dram[bass.ds(b, 1), :, T:T + S].rearrange("o p i -> p (o i)"),
                             qT[:, bass.ds(b * S, S)]).then_inc(q_stored, 16)

            def load_queries(b, turns, slots_used):
                q_now = q_dram[bass.ds(b, 1)]
                for n, blk in turns:
                    if slots_used:
                        sp.wait_ge(q_rel_ready, b * TB + n + 1)
                    for i in range(QT):
                        sp.dma_start(q_rep[HD * i:HD * i + HD, n % 2, :, :],
                                     q_now[:, :, (blk + 1) * T:(blk + 2) * T]
                                     .rearrange("o (h d) i -> d (o h) i", d=HD)).then_inc(q_rep_loaded[n % 2], 16)

            store_queries(0)
            sp.wait_ge(q_stored, 16)
            load_queries(0, blocks()[:2], False)
            with sp.Fori(1, B) as b:
                store_queries(b)
            sp.wait_ge(q_stored, 16 * B)
            sp.wait_ge(ctx_v_copied, 1)
            sp.dma_start(v_dram.rearrange("b h j d -> j (b h) d"),
                         ctx_v[:].rearrange("j (g d) -> j g d", d=HD)).then_inc(ctx_v_stored, 16)
            load_queries(0, blocks()[2:], True)
            sp.wait_ge(ctx_v_stored, 16)
            for b in range(B):
                v_all = v_dram[b].rearrange("h j d -> (h j) d")
                sp.dma_start(v_rows[:, b, 0:XC - 1, :],
                             v_all[0:(XC - 1) * T].rearrange("(c p) d -> p c d", p=T)).then_inc(v_rows_loaded, 16)
                sp.dma_start(v_rows[0:TAIL, b, XC - 1, :], v_all[(XC - 1) * T:XW]).then_inc(v_rows_loaded, 16)
            with sp.Fori(1, B) as b:
                load_queries(b, blocks(), True)

            with sp.Fori(0, B) as b:
                sp.wait_ge(e_added, (b + 1) * (E + 1) + ONE)
                sp.dma_start(out[bass.ds(b, 1)].rearrange("o (t p) d -> p (o t) d", p=T),
                             X[:, bass.ds(b * TB, TB), :]).then_inc(out_stored, 16)
            sp.wait_ge(out_stored, 16 * B)

        @block.gpsimd
        def _(pool):
            pool.sem_inc(h_sq, ONE)
            nc.gpsimd.memset(V_now[:], 0.0).then_inc(const_ready, 1)
            nc.gpsimd.memset(pt_diag[:], 0.0).then_inc(const_ready, 1)
            pool.wait_ge(b_loaded, 16)
            with pool.Fori(0, B) as b:
                pool.wait_ge(ln_var, b + 1)
                nc.gpsimd.tensor_tensor(X[:, bass.ds(b * TB, TB), :], X[:, bass.ds(b * TB, TB), :],
                                        cb["bo"].unsqueeze(1).to_broadcast([128, TB, D]),
                                        ALU.add).then_inc(bias_added, 1)

            def build_queries(b, first):
                for n, blk in blocks():
                    slot = n % 2
                    if not (first and n < 2):
                        pool.wait_ge(scores_ready, b * STEPS + (n - 1) * BS)
                    nc.gpsimd.tensor_tensor(
                        q_blk[:, slot],
                        qT[:, bass.ds(b * S + blk * T, T)].unsqueeze(2).to_broadcast([128, T, H]),
                        ca["head_mask"].unsqueeze(1).to_broadcast([128, T, H]),
                        ALU.mult).then_inc(q_blk_ready, 1)
                    pool.wait_ge(q_rep_loaded[slot], (b * 2 + n // 2 + 1) * 16 * QT)
                    nc.gpsimd.tensor_tensor(
                        q_rel[0:QT * HD, slot].rearrange("p (g i) h -> p g i h", i=QT),
                        q_rep[:, slot].rearrange("p h (g i) -> p g i h", i=QT),
                        ca["query_mask"][0:QT * HD].unsqueeze(1).unsqueeze(3)
                        .to_broadcast([QT * HD, T // QT, QT, H]),
                        ALU.mult).then_inc(q_rel_ready, 1)
                    if first and n == 0:
                        pool.wait_ge(qT_ready, PRO)
                        pool.wait_ge(psO_read, PRO)
                    if n == 1:
                        pool.wait_ge(psO_ready, PRO + b * TB)
                        for i in range(HQ):
                            ins = nc.gpsimd.tensor_copy(
                                V_now[:].rearrange("p t (q r) c -> p t q r c", r=HQ)[:, :, :, i, i * HD:i * HD + HD],
                                V[:, bass.ds(b * TB, TB)].rearrange("p t (q r) d -> p t q r d", r=HQ)[:, :, :, i, :])
                        ins.then_inc(v_ready, 1)

            pool.wait_ge(const_ready, 2)
            pool.wait_ge(qT_ready, 1 + ONE)
            build_queries(0, True)
            with pool.Fori(1, B) as b:
                build_queries(b, False)

            def prepare(b):
                pool.wait_ge(ln_var, b + B + 1)
                nc.gpsimd.tensor_tensor(X[:, bass.ds(b * TB, TB), :], X[:, bass.ds(b * TB, TB), :],
                                        cb["xbp"].unsqueeze(1).to_broadcast([128, TB, D]),
                                        ALU.add).then_inc(bias_added, 1)
            def element(b, more):
                if not (isinstance(b, int) and b == 0):
                    pool.wait_ge(xs_ready, b * TB)
                nc.gpsimd.tensor_tensor(x_key, khT[:, bass.ds(b * M, M)].unsqueeze(1).to_broadcast([128, H, M]),
                                        ca["head_mask"].unsqueeze(2).to_broadcast([128, H, M]),
                                        ALU.mult).then_inc(x_key_ready, 1)
                pool.wait_ge(psO_ready, PRO + B * TB + b * TB)
                for rows, cs in ((T, slice(0, XC - 1)), (TAIL, slice(XC - 1, XC))):
                    n = cs.stop - cs.start
                    nc.gpsimd.tensor_tensor(
                        x_v[0:rows, cs].rearrange("p c (h d) -> p c h d", d=HD),
                        v_rows[0:rows, bass.ds(b, 1), cs, :].rearrange("p o c d -> p (o c) d")
                        .unsqueeze(2).to_broadcast([rows, n, H, HD]),
                        cb["chunk_head"][0:rows].rearrange("p (c h) -> p c h", h=H)[:, cs]
                        .unsqueeze(3).to_broadcast([rows, n, H, HD]),
                        ALU.mult).then_inc(x_v_ready, 1)
                if more:
                    prepare(b + 1)

            prepare(0)
            pool.wait_ge(kh_copied, 1)
            pool.wait_ge(v_rows_loaded, 2 * B * 16)
            element(0, True)
            with pool.Fori(1, B - 1) as b:
                element(b, True)
            element(B - 1, False)

            def experts(b, more):
                for e in range(E + 1):
                    pool.wait_ge(h_relu, b * (E + 1) + e + 1 + ONE)
                    pool.wait_ge(e_ready, b * (E + 1) + max(e - 1, 0) + ONE)
                    nc.gpsimd.tensor_tensor(hidden[:, e % 2], relu[:, e % 2], relu[:, e % 2],
                                            ALU.mult).then_inc(h_sq, 1)

            with pool.Fori(0, B - 1) as b:
                experts(b, True)
            experts(B - 1, False)

        @block.scalar
        def _(act):
            for started in (*psT_read, scores_read, h_relu):
                act.sem_inc(started, ONE)
            def seed(i, st, groups):
                nc.scalar.activation(st[:, 3, 0:groups], st[:, 2, 0:groups], ACT.Ln).then_inc(seed_log, 1)
                act.wait_ge(seed_log, i + 1)
                nc.scalar.activation(st[:, 5, 0:groups], st[:, 3, 0:groups], ACT.Exp, scale=-0.5).then_inc(seeded, 1)

            act.wait_ge(c_tr, 1)
            nc.scalar.activation(ctxT, psM[:, 0:B * M], ACT.Copy).then_inc(c_copied, 1)
            act.wait_ge(ln_var, 1)
            seed(0, stat, TB)
            act.wait_ge(c_kv, 1)
            nc.scalar.activation(ctx_v[:], psS[0:M, 3, :], ACT.Copy).then_inc(ctx_v_copied, 1)

            def project(b, more):
                for half in range(2):
                    act.wait_ge(psT_ready[half], b + 1 + ONE)
                    if half == 0:
                        act.wait_ge(psO_ready, b + ONE)
                    nc.scalar.activation(xnT[:, half * 256:half * 256 + 256], psT[:, half, 0:256],
                                         ACT.Copy).then_inc(psT_read[half], 1)
                if more:
                    act.wait_ge(ln_var, b + 2)
                    seed(b + 1, stat, TB)
                act.wait_ge(k_ready, b + 1)
                nc.scalar.activation(kT[:, bass.ds(b * S, S)], psS[:, 1, :], ACT.Identity,
                                     bias=ca["bk"]).then_inc(scores_read, 1)

            with act.Fori(0, B - 1) as b:
                project(b, True)
            project(B - 1, False)
            act.wait_ge(hn_var, 1)
            seed(B, k_stat, TB * H)

            with act.Fori(0, B) as b:
                for n, blk in blocks():
                    for u in range(BS):
                        s = n * BS + u
                        wide = width(blk, u)
                        act.wait_ge(max_ready, b * STEPS + s + 1)
                        k = last_unit(s - 4)
                        act.wait_ge(psT_ready[k % 2], PRO + b * (UNITS // 2) + k // 2 + 1)
                        for i in range(2):
                            ins = nc.scalar.activation(prob[:, s % 4, i, 0:wide], psS[:, 2 * (s % 2) + i, 0:wide],
                                                       ACT.Exp, bias=neg_max[:, s % 2, i:i + 1],
                                                       accum_out=row_sum[:, n % 2, 2 * u + i:2 * u + i + 1])
                        ins.then_inc(scores_read, 1)

            def front_copy(b, i, dst):
                n = front_at(b, i)
                act.wait_ge(psT_ready[i % 2], n + 1)
                if i == 2:
                    ins = nc.scalar.activation(dst, psT[:, i % 2, :], ACT.Identity, scale=cb["ln_g"], bias=cb["ln_b"])
                else:
                    ins = nc.scalar.activation(dst, psT[:, i % 2, :], ACT.Copy)
                ins.then_inc(psT_read[i % 2], 1)

            act.wait_ge(kh_tr, 1)
            nc.scalar.activation(khT, psM[:, 0:B * M], ACT.Identity, scale=cb["ln_g"],
                                 bias=cb["ln_b"]).then_inc(kh_copied, 1)
            act.wait_ge(ln_var, B + 1)
            seed(B + 1, stat, TB)
            front_copy(None, 0, xnT[:])
            front_copy(None, 1, x_q2)
            act.wait_ge(hn_var, 2)
            seed(B + 2, stat, TB * H)
            front_copy(None, 2, x_qT)

            def x_exp(b, t):
                act.wait_ge(xs_shifted, b * TB + t + 1 + ONE)
                nc.scalar.activation(x_prob[t % 2], x_prob[t % 2], ACT.Exp).then_inc(xs_exp, 1)

            def element(b, more):
                for t in range(TB):
                    if more and t == 1:
                        front_copy(b, 0, xnT[:])
                    act.wait_ge(psO_ready, PRO + B * TB + b * TB + t - 1)
                    for g, chunks in enumerate(GROUPS):
                        act.wait_ge(psT_ready[bank(t, g)], group_at(b, t, g) + 1)
                        whole = len(chunks) - (chunks[-1] == XC - 1)
                        ps = psT[:, bank(t, g), :].rearrange("p (c i) -> p c i", i=T)
                        ins = nc.scalar.activation(x_pT[t % 2][:, chunks[0]:chunks[0] + whole, :],
                                                   ps[:, 0:whole, :], ACT.Copy)
                        if whole < len(chunks):
                            ins = nc.scalar.activation(x_pT[t % 2][0:TAIL, XC - 1, :], ps[0:TAIL, whole, :], ACT.Copy)
                        ins.then_inc(psT_read[bank(t, g)], 1)
                    if t == 0:
                        act.wait_ge(ln_var, B + b + 2)
                        seed(b * 2 + B + 3, stat, TB)
                    if more and t == 1:
                        front_copy(b, 1, x_q2)
                    if more and t == 2:
                        act.wait_ge(hn_var, b + 3)
                        seed(b * 2 + B + 4, stat, TB * H)
                    if t + 1 < TB:
                        x_exp(b, t + 1)
                    elif more:
                        x_exp(b + 1, 0)
                    act.wait_ge(sums_ready, B * TB + b * TB + t + 1)
                    nc.scalar.activation(rec[:], psM[:, 0:T], ACT.Copy).then_inc(rec_copied, 1)
                    if more and t == 2:
                        front_copy(b, 2, x_qT)

            x_exp(0, 0)
            with act.Fori(0, B - 1) as b:
                element(b, True)
            element(B - 1, False)

            def seed_experts(b):
                act.wait_ge(ln_var, 2 * B + b + 1)
                seed(b + 3 * B + 1, stat, TB)

            def copy_tokens(b):
                act.wait_ge(transposed, b + 1)
                nc.scalar.activation(xnT_next, psO[:], ACT.Copy).then_inc(xn_copied, 1)

            def move_tokens(b):
                act.wait_ge(xn_copied, b + 1)
                nc.scalar.activation(xnT[:], xnT_next, ACT.Copy).then_inc(xn_moved, 1)
                act.wait_ge(g_ready, b + 1)
                nc.scalar.activation(r_exp, psM[:, 0:TB * E], ACT.Exp, scale=-1.0).then_inc(g_exp, 1)

            def experts(b, more):
                for e in range(E + 1):
                    act.wait_ge(h_ready, b * (E + 1) + e + 1)
                    act.wait_ge(h_sq, b * (E + 1) + max(e - 1, 0) + ONE)
                    nc.scalar.activation(relu[:, e % 2], psS[:, e % 4, :], ACT.Relu).then_inc(h_relu, 1)
                    if e == 4 and more:
                        seed_experts(b + 1)
                    if e == 7 and more:
                        copy_tokens(b + 1)
                if more:
                    move_tokens(b + 1)

            copy_tokens(0)
            move_tokens(0)
            with act.Fori(0, B - 1) as b:
                experts(b, True)
            experts(B - 1, False)

        @block.vector
        def _(dve):
            class Chain:

                def __init__(self):
                    self.base, self.n = 0, 0

                def loop(self, i, start, per):
                    self.base, self.n, self.per = start + i * per, 0, per

                def done(self):
                    assert self.n == self.per, self.n

                def link(self, ins):
                    self.n += 1
                    ins.then_inc(vec_step, 1)
                    dve.wait_ge(vec_step, self.base + self.n)

            c = Chain()
            LN, HN = 8, 8
            v = nc.vector

            def refine(st, groups, i):
                var, guess, t = st[:, 2, 0:groups], st[:, 5, 0:groups], st[:, 1, 0:groups]
                dve.wait_ge(seeded, i + 1)
                c.link(v.scalar_tensor_tensor(out=t, in0=var, scalar=-0.5, in1=guess, op0=ALU.mult, op1=ALU.mult))
                c.link(v.tensor_tensor(t, t, guess, ALU.mult))
                c.link(v.scalar_tensor_tensor(out=st[:, 3, 0:groups], in0=t, scalar=1.5, in1=guess,
                                              op0=ALU.add, op1=ALU.mult))

            def ln_centre(b):
                xt = X[:, bass.ds(b * TB, TB), :]
                c.link(v.reduce_sum(stat[:, 0, 0:TB], xt, AX_X))
                c.link(v.tensor_scalar(stat[:, 4, 0:TB], stat[:, 0, 0:TB], 1.0 / D, None, ALU.mult))
                c.link(v.tensor_tensor(xc[:], xt, stat[:, 4, 0:TB].unsqueeze(2).to_broadcast([128, TB, D]),
                                       ALU.subtract))

            def ln_variance():
                c.link(v.tensor_tensor(sq[:], xc[:], xc[:], ALU.mult))
                c.link(v.reduce_sum(stat[:, 1, 0:TB], sq[:], AX_X))
                v.tensor_scalar(stat[:, 2, 0:TB], stat[:, 1, 0:TB], 1.0 / D, EPS,
                                ALU.mult, ALU.add).then_inc(ln_var, 1)

            def ln_scale(seeds, stage_used=None):
                refine(stat, TB, seeds)
                if stage_used is not None:
                    dve.wait_ge(psT_ready[1], stage_used)
                v.tensor_tensor(stage[:], xc[:], stat[:, 3, 0:TB].unsqueeze(2).to_broadcast([128, TB, D]),
                                ALU.mult).then_inc(ln_done, 1)

            def layer_norm(b, seeds, stage_used=None):
                ln_centre(b)
                ln_variance()
                ln_scale(seeds, stage_used)

            def head_centre(src, xc_, sq_, st, parts, groups):
                mean = st[:, 4, 0:groups].unsqueeze(2).to_broadcast([parts, groups, HD])
                c.link(v.reduce_sum(st[:, 0, 0:groups], heads(src), AX_X))
                c.link(v.tensor_scalar(st[:, 4, 0:groups], st[:, 0, 0:groups], 1.0 / HD, None, ALU.mult))
                c.link(v.tensor_tensor(heads(xc_), heads(src), mean, ALU.subtract))
                c.link(v.tensor_tensor(sq_, xc_, xc_, ALU.mult))
                c.link(v.reduce_sum(st[:, 1, 0:groups], heads(sq_), AX_X))
                v.tensor_scalar(st[:, 2, 0:groups], st[:, 1, 0:groups], 1.0 / HD, EPS,
                                ALU.mult, ALU.add).then_inc(hn_var, 1)

            def head_scale(dst, xc_, st, parts, groups, seeds):
                refine(st, groups, seeds)
                v.tensor_tensor(heads(dst), heads(xc_),
                                st[:, 3, 0:groups].unsqueeze(2).to_broadcast([parts, groups, HD]),
                                ALU.mult).then_inc(hn_done, 1)

            def heads(ap):
                return ap.rearrange("p (g d) -> p g d", d=HD)

            for started in (qT_ready, psO_read, y_added, xs_shifted, e_added):
                dve.sem_inc(started, ONE)
            dve.wait_ge(a_loaded, 16)
            for slot in range(2):
                rows = slice(QT * HD, QT * HD + QT)
                v.tensor_copy(
                    q_rel[rows, slot].rearrange("p (g i) h -> p g i h", i=QT),
                    ca["query_mask"][rows].unsqueeze(1).unsqueeze(3).to_broadcast([QT, T // QT, QT, H]),
                ).then_inc(q_rel_ready, 1)
            v.tensor_scalar(rel0[:], ca["rel"][0:HD, :], ca["rel"][0:HD, 0:1], None,
                            ALU.subtract).then_inc(rel0_ready, 1)
            dve.wait_ge(x_loaded, 16)

            def project(b):
                dve.wait_ge(q_ready, b + 1)
                v.tensor_scalar(qT[:, bass.ds(b * S, S)], psS[:, 0, :], ca["bq"], SCALE,
                                ALU.add, ALU.mult).then_inc(qT_ready, 1)
                dve.wait_ge(psO_ready, b + 1 + ONE)
                v.tensor_tensor(V[:, bass.ds(b * TB, TB), :, :].rearrange("p t h d -> p t (h d)"),
                                psO[:].rearrange("p (t f) -> p t f", t=TB),
                                ca["bv"].unsqueeze(1).to_broadcast([128, TB, D]), ALU.add).then_inc(psO_read, 1)

            HALF = 5
            c.loop(0, 0, LN + HALF)
            layer_norm(0, 0)
            dve.wait_ge(c_kv, 1)
            head_centre(psS[0:M, 2, :], k_c, k_sq, k_stat, M, TB * H)
            c.done()
            with dve.Fori(1, B) as b:
                c.loop(b, HALF, LN)
                layer_norm(b, b, b + ONE)
                project(b - 1)
                c.done()
            project(B - 1)
            c.loop(0, HALF + LN * B, HN - HALF)
            head_scale(ctx_k[:], k_c, k_stat, M, TB * H, B)
            c.done()

            def finish(k):
                dve.wait_ge(sums_ready, k + 1)
                c.link(v.reciprocal(rec[:], psM[:, 0:T]))
                dve.wait_ge(psO_ready, PRO + k + 1)
                v.tensor_tensor(oT[:], psO[:, 0:T], rec[:], ALU.mult).then_inc(psO_read, 1)

            def add_y(k, tile):
                dve.wait_ge(y_ready, k + 1)
                xt = X[:, bass.ds(tile, 1), :].rearrange("p o d -> p (o d)")
                v.tensor_tensor(xt, psM[:, T:2 * T], xt, ALU.add).then_inc(y_added, 1)

            dve.wait_ge(bias_added, B)
            dve.wait_ge(const_ready, 2)
            with dve.Fori(0, B) as b:
                c.loop(b, LN * B + HN, TB)

                def copy_units(s, part=slice(None)):
                    n, u = divmod(s, BS)
                    blk = ORDER[n]
                    for i, js in list(enumerate(units(blk)))[part]:
                        if u == 0 and i == 0:
                            dve.wait_ge(psO_ready, PRO + b * TB + n - 1)
                        k = first_unit[n, u] + i
                        dve.wait_ge(psT_ready[k % 2], PRO + b * (UNITS // 2) + k // 2 + 1)
                        if js is None:
                            w = width(0, u)
                            dst = pt_diag[0:w, n % 2, :, 2 * QT * u:2 * QT * (u + 1)].rearrange("p h i -> p i h")
                            src = psT[0:w, k % 2, 0:256].rearrange("p (i h) -> p i h", h=H)
                        else:
                            dst = pt_full[n % 2][:, js[0]:js[-1] + 1, :, 2 * QT * u:2 * QT * (u + 1)]\
                                .rearrange("p j h i -> p j i h")
                            src = psT[:, k % 2, 0:256 * len(js)].rearrange("p (j i h) -> p j i h", h=H, i=2 * QT)
                        v.tensor_copy(dst, src).then_inc(psT_read[k % 2], 1)

                def spread_sums(n):
                    dve.wait_ge(scores_read, PRO + b * STEPS + (n + 1) * BS)
                    v.tensor_tensor(spread[:].rearrange("p (t i) -> p t i", i=QT),
                                    row_sum[:, n % 2, :].unsqueeze(2).to_broadcast([128, 2 * BS, QT]),
                                    ca["row_query"].unsqueeze(1).to_broadcast([128, 2 * BS, QT]),
                                    ALU.mult).then_inc(spread_ready, 1)

                for n, blk in blocks():
                    for u in range(BS):
                        s = n * BS + u
                        wide = width(blk, u)
                        if n and u == 2:
                            spread_sums(n - 1)
                        if n and u == BS - 2:
                            finish(b * TB + n - 1)
                        if n > 1 and u == 0:
                            add_y(b * TB + n - 2, b * TB + ORDER[n - 2])
                        if s >= 2:
                            copy_units(s - 2, slice(0, -1))
                        dve.wait_ge(scores_ready, b * STEPS + s + 1)
                        v.tensor_reduce(neg_max[:, s % 2], psS[:, 2 * (s % 2):2 * (s % 2) + 2, 0:wide],
                                        AX_X, ALU.max, negate=True).then_inc(max_ready, 1)
                        if s >= 2:
                            copy_units(s - 2, slice(-1, None))
                add_y(b * TB + TB - 2, b * TB + ORDER[-2])
                copy_units(STEPS - 2)
                copy_units(STEPS - 1)
                spread_sums(TB - 1)
                finish(b * TB + TB - 1)
                add_y(b * TB + TB - 1, b * TB + ORDER[-1])
                c.done()

            xc_flat, sq_flat = (a[:].rearrange("p t d -> p (t d)") for a in (xc, sq))

            def queries_centre(b):
                dve.wait_ge(psT_read[1], front_at(b, 1) + 1)
                head_centre(x_q2, xc_flat, sq_flat, stat, 128, TB * H)

            START = LN * B + HN + TB * B
            c.loop(0, START, LN + HN)
            ln_centre(0)
            ln_variance()
            ln_scale(B + 1)
            queries_centre(None)
            head_scale(x_q, xc_flat, stat, 128, TB * H, B + 2)
            c.done()
            START += LN + HN

            def shift(b, t):
                dve.wait_ge(xs_ready, b * TB + t + 1)
                sc = psS[:, :, 0:XG * M].rearrange("p g (h j) -> p g h j", h=XG)
                c.link(v.tensor_reduce(x_max, sc, AX_X, ALU.max, negate=True))
                v.tensor_tensor(x_prob[t % 2].rearrange("p (g h) j -> p g h j", h=XG), sc,
                                x_max.rearrange("p (g h) -> p g h", h=XG).unsqueeze(3)
                                .to_broadcast([128, H // XG, XG, M]), ALU.add).then_inc(xs_shifted, 1)

            def element(b, more):
                for t in range(TB):
                    k = B * TB + b * TB + t
                    if t == 0:
                        ln_centre(b + 1 if more else 0)
                        ln_variance()
                    if t + 1 < TB:
                        shift(b, t + 1)
                    elif more:
                        shift(b + 1, 0)
                    dve.wait_ge(xs_exp, b * TB + t + 1)
                    c.link(v.reduce_sum(x_sum, x_prob[t % 2], AX_X))
                    c.link(v.reciprocal(x_sum, x_sum))
                    v.tensor_copy(spread[:].rearrange("p (h d) -> p h d", h=H),
                                  x_sum.unsqueeze(2).to_broadcast([128, H, HD])).then_inc(spread_ready, 1)
                    if t:
                        add_y(k - 1, b * TB + t - 1)
                    if t == 0:
                        ln_scale(b * 2 + B + 3)
                    if t == 2 and more:
                        head_scale(x_q, xc_flat, stat, 128, TB * H, b * 2 + B + 4)
                    dve.wait_ge(rec_copied, b * TB + t + 1)
                    dve.wait_ge(psO_ready, PRO + k + 1)
                    v.tensor_tensor(oT[:], psO[:, 0:T], rec[:], ALU.mult).then_inc(psO_read, 1)
                    if t == 0 and more:
                        dve.wait_ge(bias_added, B + b + 2)
                    if t == 1 and more:
                        queries_centre(b)
                add_y(B * TB + b * TB + TB - 1, b * TB + TB - 1)

            c.loop(0, START, 1)
            shift(0, 0)
            c.done()
            START += 1
            dve.wait_ge(bias_added, B + 1)
            with dve.Fori(0, B - 1) as b:
                c.loop(b, START, 3 * TB + LN + HN)
                element(b, True)
                c.done()
            START += (B - 1) * (3 * TB + LN + HN)
            c.loop(0, START, 3 * TB - 1 + LN)
            element(B - 1, False)
            c.done()
            START += 3 * TB - 1 + LN

            def route(b):
                dve.wait_ge(g_exp, b + 1)
                c.link(v.tensor_tensor(r_z.rearrange("p (t e) -> p t e", t=TB),
                                       psM[:, 0:TB * E].rearrange("p (t e) -> p t e", t=TB),
                                       cb["lb"].unsqueeze(1).to_broadcast([128, TB, E]), ALU.add))
                mine = r_z.unsqueeze(2).to_broadcast([128, TB * E, E])
                other = r_z.rearrange("p (t e) -> p t e", t=TB).unsqueeze(2).to_broadcast([128, TB, E, E])
                mine4 = mine.rearrange("p (t e) f -> p t e f", t=TB)
                c.link(v.tensor_tensor(r_gt.rearrange("p (t e f) -> p t e f", t=TB, e=E), mine4, other, ALU.is_lt))
                c.link(v.tensor_tensor(r_eq.rearrange("p (t e f) -> p t e f", t=TB, e=E), mine4, other, ALU.is_equal))
                before = cb["before"].unsqueeze(1).to_broadcast([128, TB, E * E])
                eq = r_eq.rearrange("p (t f) -> p t f", t=TB)
                c.link(v.tensor_tensor(eq, eq, before, ALU.mult))
                c.link(v.tensor_tensor(r_gt, r_gt, r_eq, ALU.add))
                c.link(v.reduce_sum(r_rank, r_gt.rearrange("p (g f) -> p g f", f=E), AX_X))
                c.link(v.tensor_scalar(r_sig, r_exp, 1.0, None, ALU.add))
                c.link(v.reciprocal(r_sig, r_sig))
                c.link(v.scalar_tensor_tensor(out=r_w, in0=r_rank, scalar=2.0, in1=r_sig,
                                              op0=ALU.is_lt, op1=ALU.mult))
                w3 = r_w.rearrange("p (t e) -> p t e", t=TB)
                c.link(v.reduce_sum(r_sum, w3, AX_X))
                c.link(v.tensor_scalar(r_sum, r_sum, 1e-6, None, ALU.add))
                v.reciprocal(r_inv, r_sum).then_inc(we_ready, 1)
                dve.wait_ge(we_ready, 2 * b + 1)
                v.tensor_tensor(r_we.rearrange("p (t e) -> p t e", t=TB), w3,
                                r_inv.unsqueeze(2).to_broadcast([128, TB, E]), ALU.mult).then_inc(we_ready, 1)

            def experts(b, more):
                dve.wait_ge(we_ready, 2 * b + 2)
                for e in range(E + 1):
                    dve.wait_ge(e_ready, b * (E + 1) + e + 1 + ONE)
                    dve.wait_ge(e_added, b * (E + 1) + e + ONE)
                    if e == E:
                        xt = X[:, bass.ds(b * TB, TB), :]
                        v.tensor_tensor(xt, psT[:, e % 2, :].rearrange("p (t d) -> p t d", t=TB), xt,
                                        ALU.add).then_inc(e_added, 1)
                        continue
                    for t in range(TB):
                        xt = X[:, bass.ds(b * TB + t, 1), :].rearrange("p o d -> p (o d)")
                        ins = v.scalar_tensor_tensor(out=xt, in0=psT[:, e % 2, t * T:t * T + T],
                                                     scalar=r_we[:, t * E + e:t * E + e + 1], in1=xt,
                                                     op0=ALU.mult, op1=ALU.add)
                    ins.then_inc(e_added, 1)
                    if e == 0 and more:
                        ln_centre(b + 1)
                    if e == 1 and more:
                        ln_variance()
                    if e == 4 and more:
                        ln_scale(b + 3 * B + 2)
                if more:
                    route(b + 1)

            c.loop(0, START, 11)
            route(0)
            c.done()
            with dve.Fori(0, B - 1) as b:
                c.loop(b, START + 11, LN + 11)
                experts(b, True)
                c.done()
            experts(B - 1, False)

        @block.tensor
        def _(pe):
            mm = nc.tensor.matmul

            for started in (*psT_ready, psO_ready, e_ready):
                pe.sem_inc(started, ONE)
            pe.wait_ge(a_loaded, 16)
            pe.wait_ge(ctx_loaded, 16)
            for b in range(B):
                ins = nc.tensor.transpose(psM[:, b * M:b * M + M], ctx_sb[:, b, :], ident[0:M, 0:M])
            ins.then_inc(c_tr, 1)
            pe.wait_ge(c_copied, 1)
            pe.wait_ge(b_loaded, 16)
            for b in range(B):
                mm(psS[0:M, 2, b * D:b * D + D], ctxT[:, b * M:b * M + M], cb["xwk"], start=True, stop=True)
            for b in range(B):
                ins = mm(psS[0:M, 3, b * D:b * D + D], ctxT[:, b * M:b * M + M], cb["xwv"], start=True, stop=True)
            ins.then_inc(c_kv, 1)

            with pe.Fori(0, B) as b:
                pe.wait_ge(ln_done, b + 1)
                for half in range(2):
                    pe.wait_ge(psT_read[half], b + ONE)
                    for i in range(2):
                        ins = nc.tensor.transpose(psT[:, half, i * T:i * T + T], stage[:, 2 * half + i, :], ident)
                    ins.then_inc(psT_ready[half], 1)
                for half in range(2):
                    pe.wait_ge(psT_read[half], b + 1 + ONE)
                pe.wait_ge(qT_ready, b + ONE)
                mm(psS[:, 0, :], ca["wq"], xnT[:], start=True, stop=True).then_inc(q_ready, 1)
                pe.wait_ge(scores_read, b + ONE)
                mm(psS[:, 1, :], ca["wk"], xnT[:], start=True, stop=True).then_inc(k_ready, 1)
                pe.wait_ge(psO_read, b + ONE)
                for t in range(TB):
                    ins = mm(psO[:, t * D:t * D + D], xnT[:, t * T:t * T + T], ca["wv"], start=True, stop=True)
                ins.then_inc(psO_ready, 1)

            def attend(quadrant, parts, last):
                n = 0
                for i in range(HQ):
                    mine = parts(quadrant * HQ + i)
                    for val, w in mine:
                        ins = mm(psO[quadrant * 32:quadrant * 32 + 32, 0:T], val, w,
                                 start=(n == 0), stop=(n == HQ * len(mine) - 1))
                        n += 1
                if last:
                    ins.then_inc(psO_ready, 1)

            def project_o(k, w):
                pe.wait_ge(psO_read, PRO + k + 1)
                mm(psM[:, T:2 * T], oT[:], w, start=True, stop=True).then_inc(y_ready, 1)

            pe.wait_ge(rel_loaded, 16 * QT)
            pe.wait_ge(hn_var, 1)
            pe.wait_ge(ctx_v_copied, 1)
            pe.wait_ge(qT_ready, PRO)
            pe.wait_ge(psO_read, PRO)
            pe.wait_ge(scores_read, PRO)
            with pe.Fori(0, B) as b:
                def scores(s, r):
                    n, u = divmod(s, BS)
                    blk = ORDER[n]
                    wide = width(blk, u)
                    if u == 0 and r == 0:
                        pe.wait_ge(q_blk_ready, b * TB + n + 1)
                        pe.wait_ge(q_rel_ready, b * TB + n + 3)
                    if r == 0:
                        pe.wait_ge(scores_read, PRO + b * STEPS + s - 1)
                    q0 = (2 * u + r) * QT
                    i0 = blk * T + q0
                    lo = max(0, i0 - P)
                    dst = psS[:, 2 * (s % 2) + r, :]
                    mm(dst[:, 0:wide], q_blk[:, n % 2, q0:q0 + QT, :].rearrange("p i h -> p (i h)"),
                       kT[:, bass.ds(b * S, wide)], start=True, stop=False)
                    ins = mm(dst[:, lo:wide],
                             q_rel[0:QT * HD + QT, n % 2, q0:q0 + QT, :].rearrange("p i h -> p (i h)"),
                             rel[0:QT * HD + QT, lo - i0 + P:wide - i0 + P], start=False, stop=True)
                    if r == 1:
                        ins.then_inc(scores_ready, 1)

                def transpose_weights(s, part=slice(None)):
                    n, u = divmod(s, BS)
                    blk = ORDER[n]
                    for i, js in list(enumerate(units(blk)))[part]:
                        if i == 0:
                            pe.wait_ge(scores_read, PRO + b * STEPS + s + 1)
                        k = first_unit[n, u] + i
                        pe.wait_ge(psT_read[k % 2], PRO + b * (UNITS // 2) + k // 2)
                        w = T if js else width(0, u)
                        for jn, j in enumerate(js or [blk]):
                            for r in range(2):
                                at = (jn * 2 + r) * T
                                ins = nc.tensor.transpose(psT[0:w, k % 2, at:at + T],
                                                          prob[:, s % 4, r, j * T:j * T + w], ident)
                        ins.then_inc(psT_ready[k % 2], 1)

                def copied(n):
                    last = first_unit[n, BS - 1] + len(units(ORDER[n])) - 1
                    for k in (last - 1, last):
                        pe.wait_ge(psT_read[k % 2], PRO + b * (UNITS // 2) + k // 2 + 1)

                def attend_block(n, quadrant):
                    blk = ORDER[n]
                    k = b * TB + n
                    if quadrant == 0:
                        if n == 0:
                            pe.wait_ge(v_ready, b + 1)
                        copied(n)
                        pe.wait_ge(psO_read, PRO + k)

                    def parts(h):
                        return [(V_now[:, j, h, :], pt_full[n % 2][:, j, h, :]) for j in range(blk)] + \
                               [(V_now[:, blk, h, :], pt_diag[:, n % 2, h, :])]

                    attend(quadrant, parts, quadrant == 3)

                def sum_rows(k):
                    pe.wait_ge(spread_ready, k + 1)
                    pe.wait_ge(y_added, k + ONE)
                    mm(psM[:, 0:T], ca["row_head"], spread[:], start=True, stop=True).then_inc(sums_ready, 1)

                for s in range(STEPS):
                    n, u = divmod(s, BS)
                    scores(s, 0)
                    if s >= 2:
                        early = min(1, len(units(ORDER[(s - 2) // BS])) - 1)
                        transpose_weights(s - 2, slice(0, early))
                    scores(s, 1)
                    if s >= 2:
                        transpose_weights(s - 2, slice(early, None))
                    if n and 2 <= u <= 5:
                        attend_block(n - 1, u - 2)
                    if n and u == 4:
                        sum_rows(b * TB + n - 1)
                    if n and u == 7:
                        project_o(b * TB + n - 1, cb["wo"])
                transpose_weights(STEPS - 2)
                transpose_weights(STEPS - 1)
                sum_rows(b * TB + TB - 1)
                for quadrant in range(4):
                    attend_block(TB - 1, quadrant)
                project_o(b * TB + TB - 1, cb["wo"])

            pe.wait_ge(y_added, B * TB + ONE)
            pe.wait_ge(hn_done, 1)
            for b in range(B):
                ins = nc.tensor.transpose(psM[:, b * M:b * M + M], ctx_k[:, b * D:b * D + D], ident[0:M, 0:M])
            ins.then_inc(kh_tr, 1)

            def front_tokens(b, k):
                pe.wait_ge(ln_done, B + k + 1)
                pe.wait_ge(psT_read[0], front_at(b, 0))
                for t in range(TB):
                    ins = nc.tensor.transpose(psT[:, 0, t * T:t * T + T], stage[:, t, :], ident)
                ins.then_inc(psT_ready[0], 1)

            def front_queries(b):
                pe.wait_ge(psT_read[0], front_at(b, 0) + 1)
                pe.wait_ge(psT_read[1], front_at(b, 1))
                for t in range(TB):
                    ins = mm(psT[:, 1, t * D:t * D + D], xnT[:, t * T:t * T + T], cb["xwq"], start=True, stop=True)
                ins.then_inc(psT_ready[1], 1)

            def front_transpose(b, k):
                pe.wait_ge(hn_done, k + 2)
                pe.wait_ge(psT_read[0], front_at(b, 2))
                for t in range(TB):
                    ins = nc.tensor.transpose(psT[:, 0, t * T:t * T + T], x_q[:, t * T:t * T + T], ident)
                ins.then_inc(psT_ready[0], 1)

            front_tokens(None, 0)
            front_queries(None)
            front_transpose(None, 0)
            pe.wait_ge(kh_copied, 1)

            def x_scores(b, t, queries_copied=None):
                if t == 0:
                    pe.wait_ge(x_key_ready, b + 1)
                    pe.wait_ge(psT_read[0], queries_copied)
                pe.wait_ge(xs_shifted, b * TB + t + ONE)
                for g in range(H // XG):
                    ins = mm(psS[:, g, 0:XG * M], x_qT[:, t * T:t * T + T],
                             x_key[:, g * XG:g * XG + XG, :].rearrange("p h j -> p (h j)"),
                             start=True, stop=True)
                ins.then_inc(xs_ready, 1)

            def element(b, more):
                for t in range(TB):
                    k = B * TB + b * TB + t
                    if t + 1 < TB:
                        x_scores(b, t + 1)
                    elif more:
                        x_scores(b + 1, 0, front_at(b, 2) + 1)
                    if t == 1 and more:
                        front_tokens(b, b + 1)
                    pe.wait_ge(xs_exp, b * TB + t + 1)
                    for g, chunks in enumerate(GROUPS):
                        pe.wait_ge(psT_read[bank(t, g)], group_at(b, t, g))
                        for i, ch in enumerate(chunks):
                            rows = TAIL if ch == XC - 1 else T
                            ins = nc.tensor.transpose(psT[0:rows, bank(t, g), i * T:i * T + T],
                                                      x_flat[t % 2][:, ch * T:ch * T + rows], ident)
                        ins.then_inc(psT_ready[bank(t, g)], 1)
                    if t:
                        project_o(k - 1, cb["xwp"])
                    if t == 1 and more:
                        front_queries(b)
                    if t == 0:
                        pe.wait_ge(x_v_ready, 2 * b + 2)
                    pe.wait_ge(psO_read, PRO + k)
                    for g, chunks in enumerate(GROUPS):
                        pe.wait_ge(psT_read[bank(t, g)], group_at(b, t, g) + 1)
                        for ch in chunks:
                            rows = TAIL if ch == XC - 1 else T
                            ins = mm(psO[:, 0:T], x_v[0:rows, ch, :], x_pT[t % 2][0:rows, ch, :],
                                     start=(ch == 0), stop=(ch == XC - 1))
                    ins.then_inc(psO_ready, 1)
                    pe.wait_ge(spread_ready, k + 1)
                    pe.wait_ge(y_added, k + ONE)
                    nc.tensor.transpose(psM[:, 0:T], spread[:], ident).then_inc(sums_ready, 1)
                    if t == 2 and more:
                        front_transpose(b, b + 1)
                project_o(B * TB + b * TB + TB - 1, cb["xwp"])

            x_scores(0, 0, AFTER + 2)
            with pe.Fori(0, B - 1) as b:
                element(b, True)
            element(B - 1, False)

            pe.wait_ge(y_added, 2 * B * TB + ONE)

            def front_experts(b):
                pe.wait_ge(ln_done, 2 * B + b + 1)
                for t in range(TB):
                    ins = nc.tensor.transpose(psO[:, t * T:t * T + T], stage[:, t, :], ident)
                ins.then_inc(transposed, 1)

            def gate(b):
                pe.wait_ge(xn_copied, b + 1)
                for t in range(TB):
                    ins = mm(psM[:, t * E:t * E + E], xnT_next[:, t * T:t * T + T], cb["gate"], start=True, stop=True)
                ins.then_inc(g_ready, 1)

            def experts(b, more):
                def up(e):
                    pe.wait_ge(h_relu, b * (E + 1) + max(e - 3, 0) + ONE)
                    mm(psS[:, e % 4, :], cb["w1"][:, e * D:e * D + D], xnT[:], start=True, stop=True)\
                        .then_inc(h_ready, 1)

                pe.wait_ge(xn_moved, b + 1)
                up(0)
                up(1)
                for e in range(E + 1):
                    if e + 2 < E + 1:
                        up(e + 2)
                    pe.wait_ge(h_sq, b * (E + 1) + e + 1 + ONE)
                    pe.wait_ge(e_added, b * (E + 1) + max(e - 1, 0) + ONE)
                    for t in range(TB):
                        ins = mm(psT[:, e % 2, t * D:t * D + D], hidden[:, e % 2, t * T:t * T + T],
                                 cb["w2"][:, e * D:e * D + D], start=True, stop=True)
                    ins.then_inc(e_ready, 1)
                    if e == 5 and more:
                        front_experts(b + 1)
                    if e == 6 and more:
                        pe.wait_ge(we_ready, 2 * b + 2)
                        gate(b + 1)

            front_experts(0)
            gate(0)
            with pe.Fori(0, B - 1) as b:
                experts(b, True)
            experts(B - 1, False)


def pack(parts, spec):
    width = sum(w for _, w in spec)
    out, at = np.zeros((128, width), np.float32), 0
    for name, w in spec:
        a = parts[name]
        out[0:a.shape[0], at:at + w] = a
        at += w
    return out


def kernel(**inputs):
    import concourse.bacc as bacc
    from concourse.bass_utils import run_bass_kernel_spmd

    a = {n: np.asarray(v) for n, v in inputs.items()}

    def rows(v):
        return np.broadcast_to(v.reshape(1, -1), (128, v.size))

    part = np.arange(128)
    head_mask = (part[:, None] // HD == np.arange(H)[None, :]).astype(np.float32)
    query_mask = np.zeros((128, QT), np.float32)
    query_mask[:QT * HD] = part[:QT * HD, None] // HD == np.arange(QT)[None, :]
    query_mask[QT * HD:QT * HD + QT] = np.eye(QT)
    before = np.broadcast_to((np.arange(E)[None, :] < np.arange(E)[:, None]).astype(np.float32).reshape(1, -1),
                             (128, E * E))
    row = np.arange(XC)[None, :] * T + part[:, None]
    chunk_head = (row[:, :, None] // M == np.arange(H)).astype(np.float32).reshape(128, XC * H)
    row_query = (part[:, None] // H == np.arange(QT)[None, :]).astype(np.float32)
    row_head = (part[:, None] % H == part[None, :] // HD).astype(np.float32)
    rel_base = np.zeros((72, RW), np.float32)
    ahead = np.arange(RW)[None, :] - P - np.arange(QT)[:, None] > 0
    rel_base[QT * HD:] = np.where(ahead, np.float32(MASKED), np.float32(0.0))

    pack_a = pack({
        "ident": np.eye(128, dtype=np.float32), "wq": a["L0_attn_Wq"], "wk": a["L0_attn_Wk"],
        "wv": a["L0_attn_Wv"], "bv": rows(a["L0_attn_bv"]), "bq": a["L0_attn_bq"].reshape(D, 1),
        "bk": a["L0_attn_bk"].reshape(D, 1), "head_mask": head_mask, "query_mask": query_mask,
        "rel": a["L0_attn_rel_key"].T, "row_query": row_query, "row_head": row_head}, PACK_A)
    pack_b = pack({
        "wo": a["L0_attn_Wo"], "bo": rows(a["L0_attn_bo"]), "xwq": a["L0_xattn_Wq"].T,
        "xwk": a["L0_xattn_Wk"].T, "xwv": a["L0_xattn_Wv"].T, "xwp": a["L0_xattn_Wp"].T,
        "xbp": rows(a["L0_xattn_bp"]), "ln_g": np.tile(a["L0_xattn_ln_g"], H).reshape(D, 1),
        "ln_b": np.tile(a["L0_xattn_ln_b"], H).reshape(D, 1), "gate": a["L0_ffn_gate_w"].T,
        "lb": rows(a["L0_ffn_lb_bias"]), "before": before, "chunk_head": chunk_head,
        "w1": np.concatenate([w.T for w in a["L0_ffn_w1"]] + [a["L0_ffn_cfc"].T], axis=1),
        "w2": np.concatenate([w.T for w in a["L0_ffn_w2"]] + [a["L0_ffn_cproj"].T], axis=1)}, PACK_B)

    nc = bacc.Bacc("TRN2", target_bir_lowering=False, num_devices=1)
    arrays = {"x": a["x"], "ctx": a["ctx_1024"], "pack_a": pack_a, "pack_b": pack_b, "rel_base": rel_base}
    arrays = {n: np.ascontiguousarray(v) for n, v in arrays.items()}
    aps = [nc.dram_tensor(n + "_dram", v.shape, mybir.dt.from_np(v.dtype), kind="ExternalInput").ap()
           for n, v in arrays.items()]
    out = nc.dram_tensor("out_dram", (B, S, D), F32, kind="ExternalOutput").ap()
    build(nc, *aps, out)
    r = run_bass_kernel_spmd(nc, [{n + "_dram": v for n, v in arrays.items()}], core_ids=[0])
    return r.results[0]["out_dram"]
```
